# Optimizing a Trainium2 kernel written in Bass

```python
import numpy as np
import jax
import jax.numpy as jnp

def _softmax(x, axis=-1):
    return jax.nn.softmax(x, axis=axis)

def _gelu(x):
    return jax.nn.gelu(x, approximate=True)

def _silu(x):
    return jax.nn.silu(x)

def _sigmoid(x):
    return jax.nn.sigmoid(x)

def _layernorm(x, axis=-1, eps=1e-05):
    m = jnp.mean(x, axis=axis, keepdims=True)
    v = jnp.var(x, axis=axis, keepdims=True)
    return (x - m) / jnp.sqrt(v + eps)

def _scatter_add(tgt, idx, src, axis=0):
    return tgt.at[idx].add(src)

def _segment_sum(src, seg, n):
    return jax.ops.segment_sum(src, seg, n)
kernel_name = 'mk_dlrm_tower_d1_rec_r8_80f78b'

def setup_inputs(seed: int=0):
    np.random.seed(seed)
    _w = jnp.asarray

    def _rec_inputs():
        import jax
        import jax.numpy as jnp
        _tk = jax.random.key(seed)
        dense_ctx = jax.random.normal(jax.random.fold_in(_tk, 190), (512, 16), jnp.float32)
        ids = jnp.stack([jax.random.randint(jax.random.fold_in(_tk, 200 + f), (512,), 0, v, jnp.int32) for f, v in enumerate([1250, 12500, 1000, 1250, 1000, 125000, 1250, 125000, 1000, 125000, 12500, 12500, 125000, 1000, 1000, 1000, 1000, 1000, 1000, 1000, 125000, 1000, 1250, 1000, 12500, 125000, 125000, 12500, 12500, 1250, 12500, 1000])], axis=1)
        tbl_0 = 0.05 * jax.random.normal(jax.random.fold_in(_tk, 500 + 0), (1250, 32), jnp.float32)
        tbl_1 = 0.05 * jax.random.normal(jax.random.fold_in(_tk, 500 + 1), (12500, 32), jnp.float32)
        tbl_2 = 0.05 * jax.random.normal(jax.random.fold_in(_tk, 500 + 2), (1000, 32), jnp.float32)
        tbl_3 = 0.05 * jax.random.normal(jax.random.fold_in(_tk, 500 + 3), (1250, 32), jnp.float32)
        tbl_4 = 0.05 * jax.random.normal(jax.random.fold_in(_tk, 500 + 4), (1000, 32), jnp.float32)
        tbl_5 = 0.05 * jax.random.normal(jax.random.fold_in(_tk, 500 + 5), (125000, 32), jnp.float32)
        tbl_6 = 0.05 * jax.random.normal(jax.random.fold_in(_tk, 500 + 6), (1250, 32), jnp.float32)
        tbl_7 = 0.05 * jax.random.normal(jax.random.fold_in(_tk, 500 + 7), (125000, 32), jnp.float32)
        tbl_8 = 0.05 * jax.random.normal(jax.random.fold_in(_tk, 500 + 8), (1000, 32), jnp.float32)
        tbl_9 = 0.05 * jax.random.normal(jax.random.fold_in(_tk, 500 + 9), (125000, 32), jnp.float32)
        tbl_10 = 0.05 * jax.random.normal(jax.random.fold_in(_tk, 500 + 10), (12500, 32), jnp.float32)
        tbl_11 = 0.05 * jax.random.normal(jax.random.fold_in(_tk, 500 + 11), (12500, 32), jnp.float32)
        tbl_12 = 0.05 * jax.random.normal(jax.random.fold_in(_tk, 500 + 12), (125000, 32), jnp.float32)
        tbl_13 = 0.05 * jax.random.normal(jax.random.fold_in(_tk, 500 + 13), (1000, 32), jnp.float32)
        tbl_14 = 0.05 * jax.random.normal(jax.random.fold_in(_tk, 500 + 14), (1000, 32), jnp.float32)
        tbl_15 = 0.05 * jax.random.normal(jax.random.fold_in(_tk, 500 + 15), (1000, 32), jnp.float32)
        tbl_16 = 0.05 * jax.random.normal(jax.random.fold_in(_tk, 500 + 16), (1000, 32), jnp.float32)
        tbl_17 = 0.05 * jax.random.normal(jax.random.fold_in(_tk, 500 + 17), (1000, 32), jnp.float32)
        tbl_18 = 0.05 * jax.random.normal(jax.random.fold_in(_tk, 500 + 18), (1000, 32), jnp.float32)
        tbl_19 = 0.05 * jax.random.normal(jax.random.fold_in(_tk, 500 + 19), (1000, 32), jnp.float32)
        tbl_20 = 0.05 * jax.random.normal(jax.random.fold_in(_tk, 500 + 20), (125000, 32), jnp.float32)
        tbl_21 = 0.05 * jax.random.normal(jax.random.fold_in(_tk, 500 + 21), (1000, 32), jnp.float32)
        tbl_22 = 0.05 * jax.random.normal(jax.random.fold_in(_tk, 500 + 22), (1250, 32), jnp.float32)
        tbl_23 = 0.05 * jax.random.normal(jax.random.fold_in(_tk, 500 + 23), (1000, 32), jnp.float32)
        tbl_24 = 0.05 * jax.random.normal(jax.random.fold_in(_tk, 500 + 24), (12500, 32), jnp.float32)
        tbl_25 = 0.05 * jax.random.normal(jax.random.fold_in(_tk, 500 + 25), (125000, 32), jnp.float32)
        tbl_26 = 0.05 * jax.random.normal(jax.random.fold_in(_tk, 500 + 26), (125000, 32), jnp.float32)
        tbl_27 = 0.05 * jax.random.normal(jax.random.fold_in(_tk, 500 + 27), (12500, 32), jnp.float32)
        tbl_28 = 0.05 * jax.random.normal(jax.random.fold_in(_tk, 500 + 28), (12500, 32), jnp.float32)
        tbl_29 = 0.05 * jax.random.normal(jax.random.fold_in(_tk, 500 + 29), (1250, 32), jnp.float32)
        tbl_30 = 0.05 * jax.random.normal(jax.random.fold_in(_tk, 500 + 30), (12500, 32), jnp.float32)
        tbl_31 = 0.05 * jax.random.normal(jax.random.fold_in(_tk, 500 + 31), (1000, 32), jnp.float32)
        _rk = jax.random.fold_in(_tk, 7)
        W_top1 = 0.0606339 * jax.random.normal(jax.random.fold_in(_tk, 801), (272, 512), jnp.float32)
        W_top2 = 0.0441942 * jax.random.normal(jax.random.fold_in(_tk, 802), (512, 256), jnp.float32)
        W_top3 = 0.0625 * jax.random.normal(jax.random.fold_in(_tk, 803), (256, 1), jnp.float32)
        b_top1 = jnp.zeros((512,), jnp.float32)
        b_top2 = jnp.zeros((256,), jnp.float32)
        return (dense_ctx, ids, tbl_0, tbl_1, tbl_2, tbl_3, tbl_4, tbl_5, tbl_6, tbl_7, tbl_8, tbl_9, tbl_10, tbl_11, tbl_12, tbl_13, tbl_14, tbl_15, tbl_16, tbl_17, tbl_18, tbl_19, tbl_20, tbl_21, tbl_22, tbl_23, tbl_24, tbl_25, tbl_26, tbl_27, tbl_28, tbl_29, tbl_30, tbl_31, W_top1, b_top1, W_top2, b_top2, W_top3)
    dense_ctx, ids, tbl_0, tbl_1, tbl_2, tbl_3, tbl_4, tbl_5, tbl_6, tbl_7, tbl_8, tbl_9, tbl_10, tbl_11, tbl_12, tbl_13, tbl_14, tbl_15, tbl_16, tbl_17, tbl_18, tbl_19, tbl_20, tbl_21, tbl_22, tbl_23, tbl_24, tbl_25, tbl_26, tbl_27, tbl_28, tbl_29, tbl_30, tbl_31, W_top1, b_top1, W_top2, b_top2, W_top3 = _rec_inputs()

    def _L0_rec_setup():
        import jax, jax.numpy as jnp
        import numpy as np
        B, N, K = (256, 32, 32)
        CIN_SIZE = [128, 128]
        key = jax.random.key(seed)
        k1, k2, k3 = jax.random.split(key, 3)
        inputs = jax.random.normal(k1, (B, N, K), dtype=jnp.float32)
        W0 = jax.random.normal(k2, (N * N, CIN_SIZE[0]), dtype=jnp.float32) * 0.04
        W1 = jax.random.normal(k3, (N * CIN_SIZE[0], CIN_SIZE[1]), dtype=jnp.float32) * 0.02
        return {'inputs': inputs, 'W0': W0, 'W1': W1}
    _L0_rec_all = _L0_rec_setup()
    _L0_rec_in = {k: v for k, v in _L0_rec_all.items() if k in ('W0', 'W1')}
    del _L0_rec_all
    return {'dense_ctx': dense_ctx, 'ids': ids, 'tbl_0': tbl_0, 'tbl_1': tbl_1, 'tbl_2': tbl_2, 'tbl_3': tbl_3, 'tbl_4': tbl_4, 'tbl_5': tbl_5, 'tbl_6': tbl_6, 'tbl_7': tbl_7, 'tbl_8': tbl_8, 'tbl_9': tbl_9, 'tbl_10': tbl_10, 'tbl_11': tbl_11, 'tbl_12': tbl_12, 'tbl_13': tbl_13, 'tbl_14': tbl_14, 'tbl_15': tbl_15, 'tbl_16': tbl_16, 'tbl_17': tbl_17, 'tbl_18': tbl_18, 'tbl_19': tbl_19, 'tbl_20': tbl_20, 'tbl_21': tbl_21, 'tbl_22': tbl_22, 'tbl_23': tbl_23, 'tbl_24': tbl_24, 'tbl_25': tbl_25, 'tbl_26': tbl_26, 'tbl_27': tbl_27, 'tbl_28': tbl_28, 'tbl_29': tbl_29, 'tbl_30': tbl_30, 'tbl_31': tbl_31, 'W_top1': W_top1, 'b_top1': b_top1, 'W_top2': W_top2, 'b_top2': b_top2, 'W_top3': W_top3, 'L0_rec_W0': _L0_rec_in['W0'], 'L0_rec_W1': _L0_rec_in['W1']}

def reference(dense_ctx, ids, tbl_0, tbl_1, tbl_2, tbl_3, tbl_4, tbl_5, tbl_6, tbl_7, tbl_8, tbl_9, tbl_10, tbl_11, tbl_12, tbl_13, tbl_14, tbl_15, tbl_16, tbl_17, tbl_18, tbl_19, tbl_20, tbl_21, tbl_22, tbl_23, tbl_24, tbl_25, tbl_26, tbl_27, tbl_28, tbl_29, tbl_30, tbl_31, W_top1, b_top1, W_top2, b_top2, W_top3, L0_rec_W0, L0_rec_W1):
    import jax
    import jax.numpy as jnp

    def _L0_rec_ref(inputs, W0, W1):
        import jax, jax.numpy as jnp
        import numpy as np
        B, N, K = (256, 32, 32)
        CIN_SIZE = [128, 128]
        b, n, k = inputs.shape
        x = inputs
        res = []
        for W in (W0, W1):
            prev = x.shape[1]
            z = jnp.einsum('bhd,bmd->bhmd', inputs, x).reshape(b, n * prev, k)
            x = jnp.einsum('bpd,pj->bjd', z, W)
            res.append(x)
        out = jnp.sum(jnp.concatenate(res, axis=1), axis=-1)
        return out
    e = jnp.stack([tbl_0[ids[:, 0]], tbl_1[ids[:, 1]], tbl_2[ids[:, 2]], tbl_3[ids[:, 3]], tbl_4[ids[:, 4]], tbl_5[ids[:, 5]], tbl_6[ids[:, 6]], tbl_7[ids[:, 7]], tbl_8[ids[:, 8]], tbl_9[ids[:, 9]], tbl_10[ids[:, 10]], tbl_11[ids[:, 11]], tbl_12[ids[:, 12]], tbl_13[ids[:, 13]], tbl_14[ids[:, 14]], tbl_15[ids[:, 15]], tbl_16[ids[:, 16]], tbl_17[ids[:, 17]], tbl_18[ids[:, 18]], tbl_19[ids[:, 19]], tbl_20[ids[:, 20]], tbl_21[ids[:, 21]], tbl_22[ids[:, 22]], tbl_23[ids[:, 23]], tbl_24[ids[:, 24]], tbl_25[ids[:, 25]], tbl_26[ids[:, 26]], tbl_27[ids[:, 27]], tbl_28[ids[:, 28]], tbl_29[ids[:, 29]], tbl_30[ids[:, 30]], tbl_31[ids[:, 31]]], axis=1)
    z = _L0_rec_ref(e, L0_rec_W0, L0_rec_W1)
    z = z.reshape(z.shape[0], -1)
    h = jnp.concatenate([z, dense_ctx], axis=1)
    h = jnp.maximum(h @ W_top1 + b_top1, 0.0)
    h = jnp.maximum(h @ W_top2 + b_top2, 0.0)
    y = h @ W_top3
    return y

_drawn_inputs = setup_inputs


def setup_inputs(seed=0):
    import zlib

    import numpy as np

    out = dict(_drawn_inputs(seed))
    spreads = {'b_top1': (0.0, 0.1), 'b_top2': (0.0, 0.1)}
    factors = {'tbl_0': 4.645,
     'tbl_1': 5.011,
     'tbl_2': 4.752,
     'tbl_3': 5.151,
     'tbl_4': 4.645,
     'tbl_5': 5.098,
     'tbl_6': 4.794,
     'tbl_7': 5.273,
     'tbl_8': 4.883,
     'tbl_9': 4.977,
     'tbl_10': 4.85,
     'tbl_11': 5.286,
     'tbl_12': 5.238,
     'tbl_13': 4.633,
     'tbl_14': 4.968,
     'tbl_15': 4.811,
     'tbl_16': 5.241,
     'tbl_17': 5.126,
     'tbl_18': 4.972,
     'tbl_19': 5.265,
     'tbl_20': 4.759,
     'tbl_21': 5.016,
     'tbl_22': 4.891,
     'tbl_23': 4.683,
     'tbl_24': 5.236,
     'tbl_25': 4.853,
     'tbl_26': 4.42,
     'tbl_27': 4.994,
     'tbl_28': 5.002,
     'tbl_29': 5.177,
     'tbl_30': 4.979,
     'tbl_31': 4.969,
     'L0_rec_W1': 8.0}
    for name, (base, spread) in spreads.items():
        noise = np.random.default_rng([zlib.crc32(name.encode()), seed]).standard_normal(out[name].shape)
        drawn = base * np.exp(spread * noise) if base else spread * noise
        out[name] = jnp.asarray(drawn.astype(out[name].dtype))
    for name, factor in factors.items():
        out[name] = (out[name] * factor).astype(out[name].dtype)
    return out
```

```python
from contextlib import ExitStack

import concourse.bass as bass
from concourse import mybir

F32 = mybir.dt.float32
F32R = mybir.dt.float32r
I32 = mybir.dt.int32
U32 = mybir.dt.uint32
ALU = mybir.AluOpType
ACT = mybir.ActivationFunctionType

P = 128
FIELDS = 32
DIM = 32
GROUP = P // FIELDS
SHIFTS = FIELDS // 2 + 1
WRAP = FIELDS + SHIFTS - 1
CIN = 128
TB = 4
COLS = TB * P
FULL = 4
UNITS = 3
RING = 4
BDW = FIELDS + 1
NHID1, NHID2 = 512, 256


def interaction_tower(nc, tables, ids, table_starts, w0_direct, w0_mirror, w1, dense, wt1, b1, wt2, b2, wt3, out):
    nb = ids.shape[1] // TB
    turns = nb // RING
    batch = nb * TB * GROUP
    assert ids.shape[0] == P and nb % RING == 0 and batch == 512

    ctx = ExitStack()
    with ctx:
        def sb(name, shape, dt=F32):
            return ctx.enter_context(nc.sbuf_tensor(name, shape, dt))

        def ps(name, shape):
            return ctx.enter_context(nc.psum_tensor(name, shape, F32))

        def sem(name):
            return ctx.enter_context(nc.semaphore(name))

        ids_raw = sb("ids_raw", [P, nb * TB], I32)
        starts = sb("starts", [P, nb * TB], I32)
        idx = sb("idx", [P, RING, TB], I32)
        emb = sb("emb", [P, RING, TB, DIM])
        embT = sb("embT", [P, RING, TB, WRAP])
        z = sb("z", [P, 2, TB, 4 * (FULL + 1), FIELDS])
        zh = sb("zh", [P, 2, FULL + 1, COLS], F32R)
        zl = sb("zl", [P, 2, FULL, COLS], F32R)
        x1c = sb("x1c", [P, 2, COLS])
        x1 = sb("x1", [P, 2, TB, CIN])
        bd = sb("bd", [P, 2, TB, GROUP, BDW])
        G = sb("G", [P, BDW, batch])
        ident = sb("ident", [P, P])
        w0d = sb("w0d", [P, FULL + 1, CIN])
        w0m = sb("w0m", [P, FULL + 1, CIN])
        w0s = sb("w0s", [P, FULL + 1, CIN])
        w0h = sb("w0h", [P, FULL + 1, CIN], F32R)
        w0l = sb("w0l", [P, FULL + 1, CIN], F32R)
        w1s = sb("w1s", [P, FIELDS, CIN])
        x2s = sb("x2s", [P, batch])
        denseT = sb("denseT", [16, batch])
        wt1s = sb("wt1s", [P, 2, NHID1])
        wt1d = sb("wt1d", [16, NHID1])
        wt2s = sb("wt2s", [P, NHID1 // P, NHID2])
        wt3s = sb("wt3s", [P, NHID2 // P])
        b1s = sb("b1s", [P, NHID1 // P])
        b2s = sb("b2s", [P, NHID2 // P])
        hid1 = sb("hid1", [P, NHID1 // P, batch])
        hid2 = sb("hid2", [P, NHID2 // P, batch])
        ys = sb("ys", [1, batch])

        zT = [ps(f"zT{n}", [P, 2, COLS]) for n in range(2)]
        x1T_ps = ps("x1T_ps", [P, COLS])
        x1_ps = ps("x1_ps", [P, TB, CIN])
        G_ps = ps("G_ps", [P, 2, 512])

        ids_in = sem("ids_in")
        idx_made = sem("idx_made")
        gathered = [sem(f"gathered{n}") for n in range(RING)]
        turned = sem("turned")
        emb_ready = sem("emb_ready")
        bd_zero = sem("bd_zero")
        bd_ones = sem("bd_ones")
        bd_ready = [sem(f"bd_ready{n}") for n in range(2)]
        ident_zero = sem("ident_zero")
        ident_ready = sem("ident_ready")
        w0_in = sem("w0_in")
        w0_summed = sem("w0_summed")
        w0_high = sem("w0_high")
        w0_ready = sem("w0_ready")
        w1_in = sem("w1_in")
        top_in = sem("top_in")
        z_made = sem("z_made")
        zT_made = sem("zT_made")
        zh_made = sem("zh_made")
        zl_made = sem("zl_made")
        x1T_made = sem("x1T_made")
        x1c_made = sem("x1c_made")
        x1_turned = sem("x1_turned")
        x1_made = sem("x1_made")
        G_made = sem("G_made")
        G_kept = sem("G_kept")
        x2_made = sem("x2_made")
        x2_kept = sem("x2_kept")
        hid1_made = sem("hid1_made")
        hid1_kept = sem("hid1_kept")
        hid2_made = sem("hid2_made")
        hid2_kept = sem("hid2_kept")
        y_made = sem("y_made")
        y_kept = sem("y_kept")
        y_out = sem("y_out")

        def unit_chunks(u):
            return [2 * u, 2 * u + 1] if u < 2 else [FULL]

        def wait_from_one(eng, semaphore, count):
            if not (isinstance(count, int) and count <= 0):
                eng.wait_ge(semaphore, count)

        block = ctx.enter_context(nc.Block())

        @block.sync
        def _(sp):
            sp.dma_start(ids_raw[:, :], ids).then_inc(ids_in, 16)
            sp.dma_start(starts[:, :], table_starts).then_inc(ids_in, 16)
            sp.dma_start(w0d[:, :, :], w0_direct).then_inc(w0_in, 16)
            sp.dma_start(w0m[:, :, :], w0_mirror).then_inc(w0_in, 16)

            def spread(turn, q):
                if isinstance(turn, int) and turn == 0 and q < 2:
                    sp.wait_ge(emb_ready, q + 1)
                else:
                    sp.wait_ge(G_made, turn * RING + q - 1)
                for i in range(GROUP):
                    part = slice(i * DIM, (i + 1) * DIM)
                    sp.dma_start(bd[part, q % 2, :, i, 0:FIELDS], embT[part, q, :, 0:FIELDS]).then_inc(bd_ready[q % 2], 16)

            sp.wait_ge(bd_zero, 1)
            spread(0, 0)
            spread(0, 1)
            sp.dma_start(w1s[:, :, :], w1.rearrange("(h m) j -> m h j", m=P)).then_inc(w1_in, 16)
            sp.dma_start(wt1s[:, :, :], wt1[0:2 * P, :].rearrange("(c p) n -> p c n", p=P)).then_inc(top_in, 16)
            sp.dma_start(wt1d[:, :], wt1[2 * P:2 * P + 16, :]).then_inc(top_in, 16)
            sp.dma_start(wt2s[:, :, :], wt2.rearrange("(c p) n -> p c n", p=P)).then_inc(top_in, 16)
            sp.dma_start(wt3s[:, :], wt3).then_inc(top_in, 16)
            sp.dma_start(b1s[:, :], b1).then_inc(top_in, 16)
            sp.dma_start(b2s[:, :], b2).then_inc(top_in, 16)
            sp.dma_start(denseT[:, :], dense).then_inc(top_in, 16)
            spread(0, 2)
            spread(0, 3)
            with sp.Fori(1, turns) as turn:
                for q in range(RING):
                    spread(turn, q)
            sp.wait_ge(y_kept, 1)
            sp.dma_start(out, ys[:, :]).then_inc(y_out, 16)
            sp.wait_ge(y_out, 16)

        @block.gpsimd
        def _(pool):
            nc.gpsimd.memset(ident[:, :], 0.0).then_inc(ident_zero, 1)
            pool.wait_ge(ids_in, 32)

            def rows_of(turn, q):
                at = bass.ds((turn * RING + q) * TB, TB)
                nc.gpsimd.tensor_tensor(idx[:, q % RING, :], ids_raw[:, at], starts[:, at], ALU.add).then_inc(idx_made, 1)

            def gather(turn, q, last=False):
                wait_from_one(pool, turned, turn * RING + q - 2)
                pool.wait_ge(idx_made, turn * RING + q + 1)
                if not last:
                    rows_of(turn, q + 1)
                for t in range(TB):
                    nc.gpsimd.indirect_dma_start(
                        emb[:, q, t, :], None, tables,
                        bass.IndirectOffsetOnAxis(ap=idx[:, q, t:t + 1].bitcast(U32), axis=0),
                    ).then_inc(gathered[q], 16)

            rows_of(0, 0)
            gather(0, 0)
            gather(0, 1)
            pool.wait_ge(ident_zero, 1)
            nc.gpsimd.affine_select(out=ident[:, :], in_=ident[:, :], compare_op=ALU.not_equal, fill=1.0,
                                    base=0, pattern=[[-1, P]], channel_multiplier=1).then_inc(ident_ready, 1)
            pool.wait_ge(w0_in, 32)
            nc.gpsimd.tensor_tensor(w0s[:, :, :], w0d[:, :, :], w0m[:, :, :], ALU.add).then_inc(w0_summed, 1)
            gather(0, 2)
            gather(0, 3)
            with pool.Fori(1, turns - 1) as turn:
                for q in range(RING):
                    gather(turn, q)
            for q in range(RING):
                gather(turns - 1, q, last=(q == RING - 1))

        @block.vector
        def _(dve):
            def turn_emb(turn, q):
                slot, turn_ = q % RING, turn + q // RING
                dve.wait_ge(gathered[slot], 16 * TB * (turn_ + 1))
                wait_from_one(dve, bd_ready[slot % 2], 16 * GROUP * (2 * turn_ + slot // 2 - 1))
                nc.vector.transpose(embT[:, slot, :, 0:FIELDS], emb[:, slot, :, :]).then_inc(turned, 1)
                dve.wait_ge(turned, turn * RING + q + 1)
                nc.vector.tensor_copy(embT[:, slot, :, FIELDS:WRAP], embT[:, slot, :, 0:WRAP - FIELDS]).then_inc(emb_ready, 1)

            def products(turn, q, u):
                s = turn * RING + q
                k0, nk, up = (8 * u, 8, 1) if u < 2 else (16, 4, 0)
                slot = q % RING
                dve.wait_ge(emb_ready, s + 1)
                wait_from_one(dve, zT_made, UNITS * (s - 2) + u + 1)
                e = embT[:, slot, :, :]
                field = bass.AP(tensor=e.tensor, offset=e.offset, ap=[e.ap[0], [WRAP, TB], [0, nk], [1, FIELDS]])
                other = bass.AP(tensor=e.tensor, offset=e.offset + k0, ap=[e.ap[0], [WRAP, TB], [up, nk], [1, FIELDS]])
                nc.vector.tensor_tensor(z[:, q % 2, :, k0:k0 + nk, :], field, other, ALU.mult).then_inc(z_made, 1)

            def low_parts(turn, q, u):
                s = turn * RING + q
                n = UNITS * q + u
                dve.wait_ge(zh_made, UNITS * s + u + 1)
                wait_from_one(dve, x1T_made, s - 1)
                if u < 2:
                    nc.vector.tensor_tensor(zl[:, q % 2, 2 * u:2 * u + 2, :], zT[n % 2][:, :, :],
                                            zh[:, q % 2, 2 * u:2 * u + 2, :].bitcast(F32), ALU.subtract).then_inc(zl_made, 1)
                else:
                    nc.vector.tensor_tensor(zh[64:P, q % 2, FULL, :], zT[n % 2][64:P, 0, :],
                                            zh[64:P, q % 2, FULL, :].bitcast(F32), ALU.subtract).then_inc(zl_made, 1)

            def step(turn, q, last=False):
                for u in range(UNITS):
                    low_parts(turn, q, u)
                    if not (last and q == RING - 1):
                        products(turn + (q + 1) // RING, (q + 1) % RING, u)
                if not (last and q >= RING - 2):
                    turn_emb(turn + (q + 2) // RING, (q + 2) % RING)

            nc.vector.memset(bd[:, :, :, :, :], 0.0).then_inc(bd_zero, 1)
            turn_emb(0, 0)
            for u in range(UNITS):
                products(0, 0, u)
            turn_emb(0, 1)
            dve.wait_ge(w0_high, 1)
            nc.vector.tensor_tensor(w0l[:, :, :], w0s[:, :, :], w0h[:, :, :].bitcast(F32), ALU.subtract).then_inc(w0_ready, 1)
            dve.wait_ge(w0_ready, 1)
            for p in (32, 96):
                nc.vector.tensor_copy(w0h[p:p + 32, FULL, :], w0l[p:p + 32, FULL, :].bitcast(F32)).then_inc(w0_ready, 1)
            dve.wait_ge(bd_zero, 1)
            for i in range(GROUP):
                nc.vector.memset(bd[i * DIM:(i + 1) * DIM, :, :, i, FIELDS:BDW], 1.0).then_inc(bd_ones, 1)
            for q in range(RING):
                step(0, q)
            with dve.Fori(1, turns - 1) as turn:
                for q in range(RING):
                    step(turn, q)
            for q in range(RING):
                step(turns - 1, q, last=True)
            dve.wait_ge(x2_made, 1)
            nc.vector.tensor_copy(x2s[:, :], x1T_ps[:, :]).then_inc(x2_kept, 1)
            dve.wait_ge(y_made, 1)
            nc.vector.tensor_copy(ys[:, :], x1_ps[0:1, 0:TB, :].rearrange("p t n -> p (t n)")).then_inc(y_kept, 1)

        @block.scalar
        def _(act):
            act.wait_ge(w0_summed, 1)
            nc.scalar.activation(w0h[:, :, :], w0s[:, :, :], ACT.Copy).then_inc(w0_high, 1)

            def high_parts(turn, q, u):
                s = turn * RING + q
                n = UNITS * q + u
                act.wait_ge(zT_made, UNITS * s + u + 1)
                wait_from_one(act, x1T_made, s - 1)
                chunks = unit_chunks(u)
                nc.scalar.activation(zh[:, q % 2, chunks[0]:chunks[-1] + 1, :], zT[n % 2][:, 0:len(chunks), :],
                                     ACT.Copy).then_inc(zh_made, 1)

            def keep_x1c(turn, q):
                s = turn * RING + q
                act.wait_ge(x1T_made, s)
                wait_from_one(act, x1_turned, s - 2)
                nc.scalar.activation(x1c[:, (q - 1) % 2, :], x1T_ps[:, :], ACT.Copy).then_inc(x1c_made, 1)

            def keep_x1(turn, q):
                s = turn * RING + q
                act.wait_ge(x1_turned, s - 1)
                wait_from_one(act, G_made, s - 3)
                nc.scalar.activation(x1[:, q % 2, :, :], x1_ps[:, :, :], ACT.Copy).then_inc(x1_made, 1)

            def keep_G(turn, q):
                s = turn * RING + q
                act.wait_ge(G_made, s - 1)
                nc.scalar.activation(
                    G[:, :, bass.ds((s - 2) * TB * GROUP, TB * GROUP)].rearrange("m h (u v) -> m u v h", u=2),
                    G_ps[:, :, 0:2 * GROUP * BDW].rearrange("m u (v h) -> m u v h", h=BDW),
                    ACT.Copy).then_inc(G_kept, 1)

            def step(turn, q, first=False, ended=False):
                if not ended:
                    high_parts(turn, q, 0)
                if not (first and q < 2):
                    keep_x1(turn, q)
                if not ended:
                    high_parts(turn, q, 1)
                if not (first and q < 1) and not (ended and q > 0):
                    keep_x1c(turn, q)
                if not ended:
                    high_parts(turn, q, 2)
                if not (first and q < 2):
                    keep_G(turn, q)

            for q in range(RING):
                step(0, q, first=True)
            with act.Fori(1, turns) as turn:
                for q in range(RING):
                    step(turn, q)
            for q in range(2):
                step(turns, q, ended=True)

            act.wait_ge(top_in, 16 * 7)
            for n in range(NHID1 // P):
                act.wait_ge(hid1_made, n + 1)
                nc.scalar.activation(hid1[:, n, :], zT[n // 2][:, n % 2, :], ACT.Relu, bias=b1s[:, n:n + 1]).then_inc(hid1_kept, 1)
            for n in range(NHID2 // P):
                act.wait_ge(hid2_made, n + 1)
                nc.scalar.activation(hid2[:, n, :], G_ps[:, n, :], ACT.Relu, bias=b2s[:, n:n + 1]).then_inc(hid2_kept, 1)

        @block.tensor
        def _(pe):
            def turn_z(turn, q, u):
                s = turn * RING + q
                n = UNITS * q + u
                pe.wait_ge(z_made, UNITS * s + u + 1)
                wait_from_one(pe, zl_made, UNITS * s + u - 1)
                for c, chunk in enumerate(unit_chunks(u)):
                    for t in range(TB):
                        rows = z[:, q % 2, t, 4 * chunk:4 * chunk + 4, :].rearrange("p k h -> p (k h)")
                        last = nc.tensor.transpose(zT[n % 2][:, c, t * P:(t + 1) * P], rows, ident[:, :])
                last.then_inc(zT_made, 1)

            def interact(turn, q, u):
                s = turn * RING + q
                slot = (q - 1) % 2
                pe.wait_ge(zl_made, UNITS * (s - 1) + u + 1)
                if u == 0:
                    wait_from_one(pe, x1c_made, s - 1)
                for c in unit_chunks(u):
                    terms = [(w0h, zh), (w0h, zl), (w0l, zh)] if u < 2 else [(w0h, zh)]
                    for k, (w, half) in enumerate(terms):
                        last = nc.tensor.matmul(x1T_ps[:, :], w[:, c, :], half[:, slot, c, :],
                                                start=(c == 0 and k == 0), stop=(u == 2))
                if u == 2:
                    last.then_inc(x1T_made, 1)

            def turn_x1(turn, q):
                s = turn * RING + q
                pe.wait_ge(x1c_made, s - 1)
                wait_from_one(pe, x1_made, s - 2)
                for t in range(TB):
                    last = nc.tensor.transpose(x1_ps[:, t, :], x1c[:, q % 2, t * P:(t + 1) * P], ident[:, :])
                last.then_inc(x1_turned, 1)

            def dot(turn, q):
                s = turn * RING + q
                slot = q % 2
                pe.wait_ge(x1_made, s - 1)
                pe.wait_ge(bd_ready[slot], 16 * GROUP * (2 * turn + q // 2))
                wait_from_one(pe, G_kept, s - 2)
                for t in range(TB):
                    v = t % 2 * GROUP * BDW
                    last = nc.tensor.matmul(G_ps[:, t // 2, v:v + GROUP * BDW], x1[:, q % 2, t, :],
                                            bd[:, slot, t, :, :].rearrange("p i h -> p (i h)"), start=True, stop=True)
                last.then_inc(G_made, 1)

            def step(turn, q, first=False, ended=False):
                started = not (first and q < 1) and not (ended and q > 0)
                if not ended:
                    turn_z(turn, q, 0)
                if not (first and q < 2):
                    turn_x1(turn, q)
                if started:
                    interact(turn, q, 0)
                if not ended:
                    turn_z(turn, q, 1)
                if started:
                    interact(turn, q, 1)
                    interact(turn, q, 2)
                if not ended:
                    turn_z(turn, q, 2)
                if not (first and q < 2):
                    dot(turn, q)

            pe.wait_ge(ident_ready, 1)
            for q in range(RING):
                if q == 1:
                    pe.wait_ge(w0_ready, 3)
                if q == 2:
                    pe.wait_ge(bd_ones, GROUP)
                step(0, q, first=True)
            with pe.Fori(1, turns) as turn:
                for q in range(RING):
                    step(turn, q)
            for q in range(2):
                step(turns, q, ended=True)

            pe.wait_ge(w1_in, 16)
            pe.wait_ge(G_kept, nb)
            for h in range(FIELDS):
                last = nc.tensor.matmul(x1T_ps[:, :], w1s[:, h, :], G[:, h, :], start=(h == 0), stop=(h == FIELDS - 1))
            last.then_inc(x2_made, 1)
            pe.wait_ge(top_in, 16 * 7)
            for n in range(NHID1 // P):
                if n == 0:
                    pe.wait_ge(x2_kept, 1)
                cols = slice(n * P, (n + 1) * P)
                bank = zT[n // 2][:, n % 2, :]
                nc.tensor.matmul(bank, wt1s[:, 0, cols], G[:, FIELDS, :], start=True, stop=False)
                nc.tensor.matmul(bank, wt1d[:, cols], denseT[:, :], start=False, stop=False)
                nc.tensor.matmul(bank, wt1s[:, 1, cols], x2s[:, :], start=False, stop=True).then_inc(hid1_made, 1)
            for n in range(NHID2 // P):
                for c in range(NHID1 // P):
                    if n == 0:
                        pe.wait_ge(hid1_kept, c + 1)
                    last = nc.tensor.matmul(G_ps[:, n, :], wt2s[:, c, n * P:(n + 1) * P], hid1[:, c, :],
                                            start=(c == 0), stop=(c == NHID1 // P - 1))
                last.then_inc(hid2_made, 1)
            for c in range(NHID2 // P):
                pe.wait_ge(hid2_kept, c + 1)
                last = nc.tensor.matmul(x1_ps[0:1, :, :].rearrange("p t n -> p (t n)"), wt3s[:, c:c + 1], hid2[:, c, :],
                                        start=(c == 0), stop=(c == NHID2 // P - 1))
            last.then_inc(y_made, 1)


def laid_out(inputs):
    import numpy as np

    n = FIELDS
    ids = np.asarray(inputs["ids"])
    tables = [np.asarray(inputs[f"tbl_{f}"]) for f in range(n)]
    starts = np.concatenate([[0], np.cumsum([t.shape[0] for t in tables])[:-1]]).astype(np.int32)
    groups = ids.shape[0] // GROUP
    w0 = np.asarray(inputs["L0_rec_W0"]).reshape(n, n, CIN)
    h = np.arange(n)
    zero = np.zeros((n, CIN), np.float32)
    direct = [w0[h, (h + k) % n] for k in range(n // 2)] + [w0[h, (h + n // 2) % n]] * 4
    mirror = [zero] + [w0[(h + k) % n, h] for k in range(1, n // 2)] + [zero] * 4
    def pack(x):
        return np.concatenate(x).reshape(FULL + 1, P, CIN).transpose(1, 0, 2).reshape(P, -1)
    return {
        "tables": np.concatenate(tables),
        "ids": ids.reshape(groups, GROUP, n).transpose(1, 2, 0).reshape(P, groups),
        "table_starts": np.repeat(np.tile(starts, GROUP)[:, None], groups, 1),
        "w0_direct": pack(direct),
        "w0_mirror": pack(mirror),
        "w1": np.asarray(inputs["L0_rec_W1"]),
        "dense": np.asarray(inputs["dense_ctx"]).T,
        "wt1": np.asarray(inputs["W_top1"]),
        "b1": np.asarray(inputs["b_top1"]).reshape(-1, P).T,
        "wt2": np.asarray(inputs["W_top2"]),
        "b2": np.asarray(inputs["b_top2"]).reshape(-1, P).T,
        "wt3": np.asarray(inputs["W_top3"]).reshape(-1, P).T,
    }


def kernel(**inputs):
    import numpy as np
    import concourse.bacc as bacc
    from concourse.bass_utils import run_bass_kernel_spmd

    nc = bacc.Bacc("TRN2", target_bir_lowering=False, num_devices=1)
    arrays, args = {}, []
    for name, a in laid_out(inputs).items():
        a = np.ascontiguousarray(a)
        arrays[f"in_{name}"] = a
        args.append(nc.dram_tensor(f"in_{name}", a.shape, mybir.dt.from_np(a.dtype), kind="ExternalInput").ap())
    batch = inputs["ids"].shape[0]
    out = nc.dram_tensor("out_y", (1, batch), F32, kind="ExternalOutput").ap()
    interaction_tower(nc, *args, out)
    r = run_bass_kernel_spmd(nc, [arrays], core_ids=[0])
    return r.results[0]["out_y"].reshape(batch, 1)
```

```python
from contextlib import ExitStack

import concourse.bass as bass
from concourse import mybir

F32 = mybir.dt.float32
F32R = mybir.dt.float32r
I32 = mybir.dt.int32
U32 = mybir.dt.uint32
ALU = mybir.AluOpType
ACT = mybir.ActivationFunctionType

P = 128
FIELDS = 32
DIM = 32
GROUP = P // FIELDS
HALF = FIELDS // 2
WRAP = FIELDS + HALF // 2
CIN = 128
TB = 4
COLS = TB * P
FULL = 4
UNITS = 3
RING = 4
BDW = FIELDS + 1
NHID1, NHID2 = 512, 256
TOPW = (2 * P * NHID1 + NHID1 * NHID2) // P // P


def interaction_tower(nc, tables, ids, table_starts, w0_direct, w0_mirror, w1, dense, topw, wt1_dense, b1, b2, wt3, scratch, out):
    nb = ids.shape[1] // TB
    turns = nb // RING
    batch = nb * TB * GROUP
    assert ids.shape[0] == P and nb % RING == 0 and batch == 512

    ctx = ExitStack()
    with ctx:
        def sb(name, shape, dt=F32):
            return ctx.enter_context(nc.sbuf_tensor(name, shape, dt))

        def ps(name, shape):
            return ctx.enter_context(nc.psum_tensor(name, shape, F32))

        def sem(name):
            return ctx.enter_context(nc.semaphore(name))

        ids_raw = sb("ids_raw", [P, nb * TB], I32)
        starts = sb("starts", [P, TB], I32)
        idx = sb("idx", [P, RING, TB], I32)
        emb = sb("emb", [P, RING, TB, DIM])
        embT = sb("embT", [P, RING, TB, WRAP])
        pairs = sb("pairs", [P, 2, 3, COLS])
        zA = sb("zA", [P, 2, TB, 2, P])
        zB = sb("zB", [P, 2, 2, COLS])
        z16 = sb("z16", [P, 2, TB // 2, P])
        zh = sb("zh", [P, 2, FULL, COLS], F32R)
        zl = sb("zl", [P, 2, FULL, COLS], F32R)
        z16s = sb("z16s", [P, 2, TB // 2, P], F32R)
        x1c = sb("x1c", [P, COLS])
        x1 = sb("x1", [P, 2, TB, CIN])
        bd = sb("bd", [P, RING, TB, GROUP, BDW])
        G = sb("G", [P, BDW, batch])
        ident = sb("ident", [P, P])
        w0h = sb("w0h", [P, FULL + 2, CIN], F32R)
        w0l = sb("w0l", [P, FULL, CIN], F32R)
        w1h = sb("w1h", [P, FIELDS, CIN], F32R)
        w1l = sb("w1l", [P, FIELDS, CIN], F32R)
        topw_h = sb("topw_h", [P, TOPW, P], F32R)
        topw_l = sb("topw_l", [P, TOPW, P], F32R)
        wt1d = sb("wt1d", [P, NHID1 // P, P], F32R)
        wt3s = sb("wt3s", [P, NHID2 // P])
        dense4 = sb("dense4", [P, NHID1 // P, P], F32R)
        b1s = sb("b1s", [P, NHID1 // P])
        b2s = sb("b2s", [P, NHID2 // P])

        topw_raw = G[:, 0:TOPW, 3 * P:4 * P]
        w0_raw = G[:, 24:30, 2 * P:3 * P]
        w0m_raw = G[:, 24:30, P:2 * P]
        w1_parts = [(0, 8, zA[:, 0, :, :, :].rearrange("p t c n -> p (t c) n")),
                    (8, 20, pairs[:, 0, :, :].rearrange("p a (b n) -> p (a b) n", n=P)),
                    (20, FIELDS, pairs[:, 1, :, :].rearrange("p a (b n) -> p (a b) n", n=P))]
        wt1d_raw = zB[:, 0, 0, :].rearrange("p (c n) -> p c n", n=P)
        dense4_raw = zB[:, 0, 1, :].rearrange("p (c n) -> p c n", n=P)
        hidden1 = zA[:, :, :, :, :].rearrange("p s t c n -> p (s t c n)").rearrange("p (c n) -> p c n", n=batch)
        hidden2 = zB[:, 0, :, :]
        ys = zB[:, 1, 0, 0:batch // P]
        high = zh[:, :, :, :].rearrange("p s c n -> p (s c) n")
        low = zl[:, :, :, :].rearrange("p s c n -> p (s c) n")
        S1, X2 = 4, 5
        Gh = zh[:, 0, :, :].rearrange("p c (g n) -> p (c g) n", g=2)
        Gl = zl[:, 0, :, :].rearrange("p c (g n) -> p (c g) n", g=2)
        G_SLOTS = 8
        G_TERMS = 2 * FIELDS

        def G_term(n):
            return G[:, n % FIELDS, n // FIELDS * batch // 2:(n // FIELDS + 1) * batch // 2]

        zAT = ps("zAT", [P, 2, COLS])
        z16T = ps("z16T", [P, 2, COLS // 2])
        x1T_ps = ps("x1T_ps", [P, 2, COLS])
        x1_ps = ps("x1_ps", [P, TB, CIN])
        G_ps = ps("G_ps", [P, 2, 512])

        hid1_ps = [zAT[:, 0, :], zAT[:, 1, :], z16T[:, :, :].rearrange("p c n -> p (c n)"), x1T_ps[:, 1, :]]

        ids_in = sem("ids_in")
        idx_made = sem("idx_made")
        first_gathered = [sem(f"first_gathered{t}") for t in range(TB)]
        first_turned = sem("first_turned")
        gathered = [sem(f"gathered{n}") for n in range(RING)]
        turned = sem("turned")
        emb_ready = sem("emb_ready")
        written = [sem(f"written{n}") for n in range(2)]
        pairs_ready = [sem(f"pairs_ready{n}") for n in range(2)]
        bd_zero = sem("bd_zero")
        bd_ones = sem("bd_ones")
        bd_ready = [sem(f"bd_ready{n}") for n in range(2)]
        ident_zero = sem("ident_zero")
        ident_ready = sem("ident_ready")
        w0_in = sem("w0_in")
        w0_summed = sem("w0_summed")
        w0_high = sem("w0_high")
        w0_ready = sem("w0_ready")
        w1_in = [sem(f"w1_in{n}") for n in range(3)]
        w1_high = sem("w1_high")
        w1_low = sem("w1_low")
        topw_in = sem("topw_in")
        topw_high = sem("topw_high")
        topw_low = sem("topw_low")
        small_in = sem("small_in")
        small_high = sem("small_high")
        small_low = sem("small_low")
        late_in = sem("late_in")
        zA_made = sem("zA_made")
        zB_made = sem("zB_made")
        z16_made = sem("z16_made")
        zT_made = sem("zT_made")
        zh_made = sem("zh_made")
        zl_made = sem("zl_made")
        x1T_made = sem("x1T_made")
        x1c_made = sem("x1c_made")
        x1_turned = sem("x1_turned")
        x1_made = sem("x1_made")
        G_made = sem("G_made")
        G_kept = sem("G_kept")
        Gh_made = sem("Gh_made")
        Gl_made = sem("Gl_made")
        s1h_made = sem("s1h_made")
        s1l_made = sem("s1l_made")
        x2_terms = sem("x2_terms")
        x2h_made = sem("x2h_made")
        x2l_made = sem("x2l_made")
        hid1_made = sem("hid1_made")
        hid1_kept = sem("hid1_kept")
        hid1h_made = sem("hid1h_made")
        hid1l_made = sem("hid1l_made")
        hid2_made = sem("hid2_made")
        hid2_kept = sem("hid2_kept")
        y_made = sem("y_made")
        y_kept = sem("y_kept")
        y_out = sem("y_out")

        def wait_from_one(eng, semaphore, count):
            if not (isinstance(count, int) and count <= 0):
                eng.wait_ge(semaphore, count)

        def block_before(turn, q, n):
            return turn + (q - n) // RING, (q - n) % RING

        TOPW_TURNS = 4
        assert TOPW_TURNS < turns - 2

        def topw_part(turn):
            n = TOPW // TOPW_TURNS
            return bass.ds((turn - 1) * n, n)

        block = ctx.enter_context(nc.Block())

        @block.sync
        def _(sp):
            sp.dma_start(ids_raw[:, :], ids).then_inc(ids_in, 16)
            sp.dma_start(starts[:, :], table_starts).then_inc(ids_in, 16)
            sp.dma_start(w0_raw, w0_direct).then_inc(w0_in, 16)
            sp.dma_start(w0m_raw, w0_mirror).then_inc(w0_in, 16)

            def write(turn, q):
                for copy in range(2):
                    if copy == 0:
                        if isinstance(turn, int) and turn + q == 0:
                            for t in range(TB):
                                sp.wait_ge(first_gathered[t], 16)
                        else:
                            sp.wait_ge(gathered[q], 16 * TB * (turn + (q > 0)))
                    else:
                        wait_from_one(sp, zB_made, turn * RING + q - 1)
                    rows = slice(FIELDS * copy, FIELDS * (copy + 1))
                    sp.dma_start(scratch[q, rows, :].rearrange("h (i n) -> i h n", i=GROUP),
                                 emb[:, q, :, :].rearrange("p t d -> p (t d)")).then_inc(written[q % 2], 16)

            def read(turn, q):
                sp.wait_ge(written[q % 2], 32 * (2 * turn + q // 2 + 1))
                block_ = scratch[q, :, :]
                for n, (first, step_) in enumerate([(0, 0), (8, COLS), (12, COLS)]):
                    src = bass.AP(tensor=block_.tensor, offset=block_.offset + first * COLS, ap=[[COLS, FIELDS], [step_, 4], [1, COLS]])
                    sp.dma_start(pairs[:, q % 2, n, :], src).then_inc(pairs_ready[q % 2], 16)

            def spread(turn, q):
                if q % 2 == 0:
                    wait_from_one(sp, G_made, turn * RING + q - 4)
                first = (q - q % 2 - 2) % RING
                for i in range(q % 2 * 2, q % 2 * 2 + 2):
                    part = slice(i * DIM, (i + 1) * DIM)
                    sp.dma_start(bd[part, first:first + 2, :, i, 0:FIELDS], embT[part, first:first + 2, :, 0:FIELDS]) \
                        .then_inc(bd_ready[first // 2], 16)

            def step(turn, q, first=False):
                write(turn, q)
                if not (first and q < 2):
                    spread(turn, q)
                read(turn, q)

            for q in range(RING):
                if q == 2:
                    sp.wait_ge(bd_zero, 1)
                step(0, q, first=True)
            sp.dma_start(topw_raw, topw).then_inc(topw_in, 16)
            sp.dma_start(wt3s[:, :], wt3).then_inc(late_in, 16)
            sp.dma_start(b1s[:, :], b1).then_inc(late_in, 16)
            sp.dma_start(b2s[:, :], b2).then_inc(late_in, 16)
            with sp.Fori(1, turns) as turn:
                for q in range(RING):
                    step(turn, q)

            def load_w1(part):
                first, end, raw = w1_parts[part]
                sp.dma_start(raw, w1.rearrange("(h m) j -> m h j", m=P)[:, first:end, :]).then_inc(w1_in[part], 16)

            sp.wait_ge(zT_made, 2 * (nb - 2) + 1)
            load_w1(0)
            sp.wait_ge(zB_made, nb - 1)
            spread(turns, 0)
            spread(turns, 1)
            load_w1(1)
            sp.wait_ge(zl_made, UNITS * (nb - 1))
            sp.dma_start(wt1d_raw, wt1_dense).then_inc(small_in, 16)
            sp.dma_start(dense4_raw, dense).then_inc(small_in, 16)
            sp.wait_ge(zB_made, nb)
            load_w1(2)
            sp.wait_ge(y_kept, 1)
            sp.dma_start(out, ys).then_inc(y_out, 16)
            sp.wait_ge(y_out, 16)

        @block.gpsimd
        def _(pool):
            nc.gpsimd.memset(ident[:, :], 0.0).then_inc(ident_zero, 1)
            pool.wait_ge(ident_zero, 1)
            nc.gpsimd.affine_select(out=ident[:, :], in_=ident[:, :], compare_op=ALU.not_equal, fill=1.0,
                                    base=0, pattern=[[-1, P]], channel_multiplier=1).then_inc(ident_ready, 1)
            pool.wait_ge(ids_in, 32)

            def rows_of(turn, q):
                at = bass.ds((turn * RING + q) * TB, TB)
                nc.gpsimd.tensor_tensor(idx[:, q % RING, :], ids_raw[:, at], starts[:, :], ALU.add).then_inc(idx_made, 1)

            def products_16(turn, q):
                s = turn * RING + q
                pool.wait_ge(emb_ready, s + 1)
                wait_from_one(pool, zT_made, 2 * (s - 1))
                for t in range(0, TB, 2):
                    e = embT[:, q, t:t + 2, :]
                    field = bass.AP(tensor=e.tensor, offset=e.offset, ap=[e.ap[0], [0, 4], [WRAP, 2], [1, HALF]])
                    other = bass.AP(tensor=e.tensor, offset=e.offset + HALF, ap=[e.ap[0], [0, 4], [WRAP, 2], [1, HALF]])
                    nc.gpsimd.tensor_tensor(z16[:, q % 2, t // 2, :].rearrange("p (c t h) -> p c t h", c=4, t=2),
                                            field, other, ALU.mult).then_inc(z16_made, 1)

            def gather(turn, q, last=False):
                wait_from_one(pool, turned, turn * RING + q - 2)
                wait_from_one(pool, written[q % 2], 32 * (2 * turn + q // 2 - 1))
                pool.wait_ge(idx_made, turn * RING + q + 1)
                if not last:
                    rows_of(turn, q + 1)
                for t in range(TB):
                    done = first_gathered[t] if isinstance(turn, int) and turn + q == 0 else gathered[q]
                    nc.gpsimd.indirect_dma_start(
                        emb[:, q, t, :], None, tables,
                        bass.IndirectOffsetOnAxis(ap=idx[:, q, t:t + 1].bitcast(U32), axis=0),
                    ).then_inc(done, 16)

            rows_of(0, 0)
            gather(0, 0)
            gather(0, 1)
            products_16(0, 0)
            gather(0, 2)
            gather(0, 3)
            def gather_turn(turn):
                for q in range(RING):
                    products_16(*block_before(turn, q, 3))
                    gather(turn, q)

            with pool.Fori(1, 2) as turn:
                gather_turn(turn)
            with pool.Fori(2, TOPW_TURNS + 2) as turn:
                gather_turn(turn)
                pool.wait_ge(topw_high, turn - 1)
                at = topw_part(turn - 1)
                nc.gpsimd.tensor_tensor(topw_l[:, at, :], topw_raw[:, at, :], topw_h[:, at, :].bitcast(F32), ALU.subtract).then_inc(topw_low, 1)
            with pool.Fori(TOPW_TURNS + 2, turns - 1) as turn:
                gather_turn(turn)
            for q in range(RING):
                products_16(*block_before(turns - 1, q, 3))
                gather(turns - 1, q, last=(q == RING - 1))
            for q in range(1, RING):
                products_16(turns - 1, q)
            for n, (first, end, raw) in enumerate(w1_parts):
                pool.wait_ge(w1_high, n + 1)
                nc.gpsimd.tensor_tensor(w1l[:, first:end, :], raw, w1h[:, first:end, :].bitcast(F32), ALU.subtract).then_inc(w1_low, 1)

        @block.vector
        def _(dve):
            def turn_emb(turn, q):
                slot, turn_ = q % RING, turn + q // RING
                dve.wait_ge(gathered[slot], 16 * TB * (turn_ + (slot > 0)))
                wait_from_one(dve, bd_ready[slot // 2], 16 * GROUP * turn_)
                nc.vector.transpose(embT[:, slot, :, 0:FIELDS], emb[:, slot, :, :]).then_inc(turned, 1)
                dve.wait_ge(turned, turn * RING + q + 1)
                nc.vector.tensor_copy(embT[:, slot, :, FIELDS:WRAP], embT[:, slot, :, 0:WRAP - FIELDS]).then_inc(emb_ready, 1)

            def products_A(turn, q, gathers=range(TB)):
                slot, first, n = q % RING, gathers[0], len(gathers)
                e = embT[:, slot, first:first + n, :]
                field = bass.AP(tensor=e.tensor, offset=e.offset, ap=[e.ap[0], [WRAP, n], [0, 8], [1, FIELDS]])
                other = bass.AP(tensor=e.tensor, offset=e.offset, ap=[e.ap[0], [WRAP, n], [1, 8], [1, FIELDS]])
                out = zA[:, q % 2, first:first + n, :, :].rearrange("p t c (k h) -> p t (c k) h", h=FIELDS)
                return nc.vector.tensor_tensor(out, field, other, ALU.mult)

            def products_B(turn, q):
                dve.wait_ge(pairs_ready[q % 2], 16 * 3 * (2 * turn + q // 2 + 1))
                for c in range(2):
                    last = nc.vector.tensor_tensor(
                        zB[:, q % 2, c, :].rearrange("p (t i d) -> p t i d", t=TB, i=GROUP),
                        pairs[:, q % 2, 0, :].rearrange("p (i t d) -> p t i d", t=TB, i=GROUP),
                        pairs[:, q % 2, 1 + c, :].rearrange("p (i t d) -> p t i d", t=TB, i=GROUP), ALU.mult)
                last.then_inc(zB_made, 1)

            def first_block():
                for t in range(TB):
                    dve.wait_ge(first_gathered[t], 16)
                    nc.vector.transpose(embT[:, 0, t, 0:FIELDS], emb[:, 0, t, :]).then_inc(turned if t == TB - 1 else first_turned, 1)
                    if t < TB - 1:
                        dve.wait_ge(first_turned, 2 * t + 1)
                    else:
                        dve.wait_ge(turned, 1)
                    nc.vector.tensor_copy(embT[:, 0, t, FIELDS:WRAP], embT[:, 0, t, 0:WRAP - FIELDS]) \
                        .then_inc(emb_ready if t == TB - 1 else first_turned, 1)
                    if t < TB - 1:
                        dve.wait_ge(first_turned, 2 * t + 2)
                    else:
                        dve.wait_ge(emb_ready, 1)
                    last = products_A(0, 0, range(t, t + 1))
                    if t == TB - 1:
                        last.then_inc(zA_made, 1)

            def low_parts(turn, q, unit):
                s = turn * RING + q
                dve.wait_ge(zh_made, UNITS * s + "ACB".index(unit) + 1)
                wait_from_one(dve, x1T_made, s - 1)
                if unit == "C":
                    low, z_, high_ = z16s[64:P, q % 2, :, :], z16T[64:P, 0, :].rearrange("p (u n) -> p u n", n=P), z16s[64:P, q % 2, :, :]
                else:
                    at = slice(0, 2) if unit == "A" else slice(2, 4)
                    low, z_, high_ = zl[:, q % 2, at, :], zAT[:, :, :] if unit == "A" else zB[:, q % 2, :, :], zh[:, q % 2, at, :]
                nc.vector.tensor_tensor(low, z_, high_.bitcast(F32), ALU.subtract).then_inc(zl_made, 1)

            def step(turn, q, first=False, last=False):
                if not (last and q == RING - 1):
                    dve.wait_ge(emb_ready, turn * RING + q + 2)
                    wait_from_one(dve, zT_made, 2 * (turn * RING + q) - 1)
                    products_A(turn + (q + 1) // RING, (q + 1) % RING).then_inc(zA_made, 1)
                if first and q == 0:
                    low_parts(turn, q, "A")
                    products_B(turn, q)
                else:
                    products_B(turn, q)
                    low_parts(turn, q, "A")
                low_parts(turn, q, "C")
                if not (last and q >= RING - 2):
                    turn_emb(turn + (q + 2) // RING, (q + 2) % RING)
                low_parts(turn, q, "B")

            nc.vector.memset(bd[:, :, :, :, :], 0.0).then_inc(bd_zero, 1)
            first_block()
            dve.wait_ge(w0_in, 32)
            nc.vector.tensor_tensor(w0_raw, w0_raw, w0m_raw, ALU.add).then_inc(w0_summed, 1)
            dve.wait_ge(w0_high, 1)
            nc.vector.tensor_tensor(w0l[:, :, :], w0_raw[:, 0:FULL, :], w0h[:, 0:FULL, :].bitcast(F32), ALU.subtract).then_inc(w0_ready, 1)
            for p in (32, 96):
                at = w0h[p:p + 32, FULL:FULL + 2, :]
                nc.vector.tensor_tensor(at, w0_raw[p:p + 32, FULL:FULL + 2, :], at.bitcast(F32), ALU.subtract).then_inc(w0_ready, 1)
            turn_emb(0, 1)
            dve.wait_ge(bd_zero, 1)
            for i in range(GROUP):
                nc.vector.memset(bd[i * DIM:(i + 1) * DIM, :, :, i, FIELDS:BDW], 1.0).then_inc(bd_ones, 1)
            for q in range(RING):
                step(0, q, first=True)
            with dve.Fori(1, turns - 1) as turn:
                for q in range(RING):
                    step(turn, q)
            for q in range(RING):
                step(turns - 1, q, last=True)

            def w1_high_part(n):
                first, end, raw = w1_parts[n]
                dve.wait_ge(w1_in[n], 16)
                nc.vector.tensor_copy(w1h[:, first:end, :], raw).then_inc(w1_high, 1)

            def G_low(first, end):
                for n in range(first, end):
                    dve.wait_ge(Gh_made, n + 1)
                    nc.vector.tensor_tensor(Gl[:, n % G_SLOTS, :], G_term(n), Gh[:, n % G_SLOTS, :].bitcast(F32), ALU.subtract).then_inc(Gl_made, 1)

            w1_high_part(0)
            w1_high_part(1)
            G_low(0, 4)
            w1_high_part(2)
            G_low(4, 8)
            dve.wait_ge(small_high, 2)
            for p, at, raw in ((32, wt1d, wt1d_raw), (96, wt1d, wt1d_raw), (64, dense4, dense4_raw)):
                rows = slice(p, p + 64 if at is dense4 else p + 32)
                nc.vector.tensor_tensor(at[rows, :, :], raw[rows, :, :], at[rows, :, :].bitcast(F32), ALU.subtract).then_inc(small_low, 1)
            G_low(8, G_TERMS)
            dve.wait_ge(s1h_made, 1)
            nc.vector.tensor_tensor(low[:, S1, :], G[:, FIELDS, :], high[:, S1, :].bitcast(F32), ALU.subtract).then_inc(s1l_made, 1)
            dve.wait_ge(x2h_made, 1)
            nc.vector.tensor_tensor(low[:, X2, :], x1T_ps[:, 0, :], high[:, X2, :].bitcast(F32), ALU.subtract).then_inc(x2l_made, 1)
            for c in range(NHID1 // P):
                dve.wait_ge(hid1_kept, c + 1)
                nc.vector.tensor_copy(high[:, c, :], hidden1[:, c, :]).then_inc(hid1h_made, 1)
                dve.wait_ge(hid1h_made, c + 1)
                nc.vector.tensor_tensor(low[:, c, :], hidden1[:, c, :], high[:, c, :].bitcast(F32), ALU.subtract).then_inc(hid1l_made, 1)
            dve.wait_ge(y_made, 1)
            nc.vector.tensor_copy(ys, x1_ps[:, 0, 0:batch // P]).then_inc(y_kept, 1)

        @block.scalar
        def _(act):
            act.wait_ge(w0_summed, 1)
            nc.scalar.activation(w0h[:, :, :], w0_raw, ACT.Copy).then_inc(w0_high, 1)

            def high_parts(turn, q, unit):
                s = turn * RING + q
                if unit == "B":
                    act.wait_ge(zB_made, s + 1)
                else:
                    act.wait_ge(zT_made, 2 * s + "AC".index(unit) + 1)
                wait_from_one(act, x1T_made, s - 1)
                if unit == "A":
                    out, z_ = zh[:, q % 2, 0:2, :], zAT[:, :, :]
                elif unit == "B":
                    out, z_ = zh[:, q % 2, 2:4, :], zB[:, q % 2, :, :]
                else:
                    out, z_ = z16s[:, q % 2, :, :], z16T[:, 0, :].rearrange("p (u n) -> p u n", n=P)
                nc.scalar.activation(out, z_, ACT.Copy).then_inc(zh_made, 1)

            def keep_x1c(turn, q):
                s = turn * RING + q
                act.wait_ge(x1T_made, s)
                wait_from_one(act, x1_turned, s - 1)
                nc.scalar.activation(x1c[:, :], x1T_ps[:, (q - 1) % 2, :], ACT.Copy).then_inc(x1c_made, 1)

            def keep_x1(turn, q):
                s = turn * RING + q
                act.wait_ge(x1_turned, s - 1)
                wait_from_one(act, G_made, s - 3)
                nc.scalar.activation(x1[:, q % 2, :, :], x1_ps[:, :, :], ACT.Copy).then_inc(x1_made, 1)

            def keep_G(turn, q):
                s = turn * RING + q
                act.wait_ge(G_made, s - 1)
                nc.scalar.activation(
                    G[:, :, bass.ds((s - 2) * TB * GROUP, TB * GROUP)].rearrange("m h (u v) -> m u v h", u=2),
                    G_ps[:, :, 0:2 * GROUP * BDW].rearrange("m u (v h) -> m u v h", h=BDW),
                    ACT.Copy).then_inc(G_kept, 1)

            def step(turn, q, first=False):
                high_parts(turn, q, "A")
                if not (first and q < 2):
                    keep_x1(turn, q)
                high_parts(turn, q, "C")
                high_parts(turn, q, "B")
                if not (first and q < 1):
                    keep_x1c(turn, q)
                if not (first and q < 2):
                    keep_G(turn, q)

            for q in range(RING):
                step(0, q, first=True)
            with act.Fori(1, TOPW_TURNS + 1) as turn:
                for q in range(RING):
                    step(turn, q)
                act.wait_ge(topw_in, 16)
                at = topw_part(turn)
                nc.scalar.activation(topw_h[:, at, :], topw_raw[:, at, :], ACT.Copy).then_inc(topw_high, 1)
            with act.Fori(TOPW_TURNS + 1, turns) as turn:
                for q in range(RING):
                    step(turn, q)

            def G_high(first, end):
                for n in range(first, end):
                    if n == 0:
                        act.wait_ge(x1T_made, nb - 1)
                        act.wait_ge(G_kept, nb // 2)
                    if n == FIELDS:
                        act.wait_ge(G_kept, nb)
                    if n >= G_SLOTS:
                        act.wait_ge(x2_terms, n - G_SLOTS + 1)
                    nc.scalar.activation(Gh[:, n % G_SLOTS, :], G_term(n), ACT.Copy).then_inc(Gh_made, 1)

            G_high(0, 2)
            keep_x1(turns, 0)
            G_high(2, 6)
            keep_x1c(turns, 0)
            G_high(6, 7)
            keep_G(turns, 0)
            keep_x1(turns, 1)
            act.wait_ge(small_in, 32)
            nc.scalar.activation(wt1d[:, :, :], wt1d_raw, ACT.Copy).then_inc(small_high, 1)
            nc.scalar.activation(dense4[:, :, :], dense4_raw, ACT.Copy).then_inc(small_high, 1)
            G_high(7, 8)
            keep_G(turns, 1)
            G_high(8, G_TERMS)
            nc.scalar.activation(high[:, S1, :], G[:, FIELDS, :], ACT.Copy).then_inc(s1h_made, 1)
            act.wait_ge(x2_terms, G_TERMS)
            nc.scalar.activation(high[:, X2, :], x1T_ps[:, 0, :], ACT.Copy).then_inc(x2h_made, 1)
            act.wait_ge(late_in, 16 * 3)
            for n in range(NHID1 // P):
                act.wait_ge(hid1_made, n + 1)
                nc.scalar.activation(hidden1[:, n, :], hid1_ps[n], ACT.Relu, bias=b1s[:, n:n + 1]).then_inc(hid1_kept, 1)
            for n in range(NHID2 // P):
                act.wait_ge(hid2_made, n + 1)
                nc.scalar.activation(hidden2[:, n, :], G_ps[:, n, :], ACT.Relu, bias=b2s[:, n:n + 1]).then_inc(hid2_kept, 1)

        @block.tensor
        def _(pe):
            def turn_A(turn, q):
                s = turn * RING + q
                pe.wait_ge(zA_made, s + 1)
                wait_from_one(pe, zl_made, UNITS * (s - 1) + 1)
                for c in range(2):
                    for t in range(TB):
                        last = nc.tensor.transpose(zAT[:, c, t * P:(t + 1) * P], zA[:, q % 2, t, c, :], ident[:, :])
                last.then_inc(zT_made, 1)

            def turn_C(turn, q):
                s = turn * RING + q
                pe.wait_ge(z16_made, 2 * s + 2)
                wait_from_one(pe, zl_made, UNITS * (s - 1) + 2)
                for t in range(TB // 2):
                    last = nc.tensor.transpose(z16T[:, 0, t * P:(t + 1) * P], z16[:, q % 2, t, :], ident[:, :])
                last.then_inc(zT_made, 1)

            def interact(turn, q, unit):
                s = turn * RING + q
                slot = (q - 1) % 2
                pe.wait_ge(zl_made, UNITS * (s - 1) + "ACB".index(unit) + 1)
                if unit == "A":
                    wait_from_one(pe, x1c_made, s - 2)
                if unit == "C":
                    for t in range(2):
                        nc.tensor.matmul(
                            x1T_ps[:, slot, :].rearrange("j (u t n) -> j u t n", u=2, t=2)[:, :, t, :],
                            w0h[:, FULL + t, :], z16s[:, slot, :, :], start=False, stop=False)
                else:
                    for c in (0, 1) if unit == "A" else (2, 3):
                        for k, (w, half) in enumerate([(w0h, zh), (w0h, zl), (w0l, zh)]):
                            last = nc.tensor.matmul(x1T_ps[:, slot, :], w[:, c, :], half[:, slot, c, :],
                                                    start=(c == 0 and k == 0), stop=(c == 3 and k == 2))
                    if unit == "B":
                        last.then_inc(x1T_made, 1)

            def turn_x1(turn, q):
                s = turn * RING + q
                pe.wait_ge(x1c_made, s - 1)
                wait_from_one(pe, x1_made, s - 2)
                for t in range(TB):
                    last = nc.tensor.transpose(x1_ps[:, t, :], x1c[:, t * P:(t + 1) * P], ident[:, :])
                last.then_inc(x1_turned, 1)

            def dot(turn, q):
                s = turn * RING + q
                slot = (q - 2) % RING
                pe.wait_ge(x1_made, s - 1)
                pe.wait_ge(bd_ready[slot // 2], 16 * GROUP * (turn + q // 2))
                wait_from_one(pe, G_kept, s - 2)
                for t in range(TB):
                    v = t % 2 * GROUP * BDW
                    last = nc.tensor.matmul(G_ps[:, t // 2, v:v + GROUP * BDW], x1[:, q % 2, t, :],
                                            bd[:, slot, t, :, :].rearrange("p i h -> p (i h)"), start=True, stop=True)
                last.then_inc(G_made, 1)

            def step(turn, q, first=False):
                started = not (first and q < 1)
                turn_A(turn, q)
                if not (first and q < 2):
                    turn_x1(turn, q)
                if started:
                    interact(turn, q, "A")
                turn_C(turn, q)
                if started:
                    interact(turn, q, "C")
                    interact(turn, q, "B")
                if not (first and q < 2):
                    dot(turn, q)

            pe.wait_ge(ident_ready, 1)
            for q in range(RING):
                if q == 1:
                    pe.wait_ge(w0_ready, 3)
                if q == 2:
                    pe.wait_ge(bd_ones, GROUP)
                step(0, q, first=True)
            with pe.Fori(1, turns) as turn:
                for q in range(RING):
                    step(turn, q)

            def products_of_halves(out, wh, wl, high_, low_, start, stop):
                nc.tensor.matmul(out, wh, high_, start=start, stop=False)
                nc.tensor.matmul(out, wl, high_, start=False, stop=False)
                return nc.tensor.matmul(out, wh, low_, start=False, stop=stop)

            def x2_term(first, end):
                for n in range(first, end):
                    h, g = n % FIELDS, n // FIELDS
                    for part, (field, _, _) in enumerate(w1_parts):
                        if n == field:
                            pe.wait_ge(w1_low, part + 1)
                    pe.wait_ge(Gl_made, n + 1)
                    products_of_halves(x1T_ps[:, 0, g * batch // 2:(g + 1) * batch // 2], w1h[:, h, :], w1l[:, h, :],
                                       Gh[:, n % G_SLOTS, :], Gl[:, n % G_SLOTS, :], h == 0, h == FIELDS - 1).then_inc(x2_terms, 1)

            turn_x1(turns, 0)
            for unit in "ACB":
                interact(turns, 0, unit)
            dot(turns, 0)
            turn_x1(turns, 1)
            x2_term(0, 2)
            dot(turns, 1)
            x2_term(2, G_TERMS)
            pe.wait_ge(s1l_made, 1)
            pe.wait_ge(topw_low, TOPW_TURNS)
            pe.wait_ge(small_low, 3)
            for n, bank in enumerate(hid1_ps):
                products_of_halves(bank, topw_h[:, n, :], topw_l[:, n, :], high[:, S1, :], low[:, S1, :], True, False)
                nc.tensor.matmul(bank, wt1d[:, n, :], dense4[:, :, :].rearrange("p c n -> p (c n)"), start=False, stop=False)
            pe.wait_ge(x2l_made, 1)
            for n, bank in enumerate(hid1_ps):
                products_of_halves(bank, topw_h[:, 4 + n, :], topw_l[:, 4 + n, :], high[:, X2, :], low[:, X2, :], False, True).then_inc(hid1_made, 1)
            for c in range(NHID1 // P):
                pe.wait_ge(hid1l_made, c + 1)
                for n in range(NHID2 // P):
                    last = products_of_halves(G_ps[:, n, :], topw_h[:, 8 + 2 * c + n, :], topw_l[:, 8 + 2 * c + n, :], high[:, c, :], low[:, c, :],
                                              c == 0, c == NHID1 // P - 1)
                    if c == NHID1 // P - 1:
                        last.then_inc(hid2_made, 1)
            pe.wait_ge(late_in, 16 * 3)
            pe.wait_ge(hid2_kept, NHID2 // P)
            for k in range(batch // P):
                for c in range(NHID2 // P):
                    last = nc.tensor.matmul(x1_ps[:, 0, k:k + 1], hidden2[:, c, k * P:(k + 1) * P], wt3s[:, c:c + 1],
                                            start=(c == 0), stop=(c == NHID2 // P - 1))
            last.then_inc(y_made, 1)


def laid_out(inputs):
    import numpy as np

    n = FIELDS
    ids = np.asarray(inputs["ids"])
    tables = [np.asarray(inputs[f"tbl_{f}"]) for f in range(n)]
    starts = np.concatenate([[0], np.cumsum([t.shape[0] for t in tables])[:-1]]).astype(np.int32)
    groups = ids.shape[0] // GROUP
    w0 = np.asarray(inputs["L0_rec_W0"]).reshape(n, n, CIN)
    h = np.arange(n)
    zero = np.zeros((n, CIN), np.float32)
    direct = [w0[h, (h + k) % n] for k in range(HALF)]
    mirror = [zero] + [w0[(h + k) % n, h] for k in range(1, HALF)]
    for rows in (direct, mirror):
        for k in range(HALF // 2, HALF, 4):
            rows[k:k + 4] = list(np.stack(rows[k:k + 4], axis=1).reshape(4, n, CIN))
    for rows, x in ((direct, w0[h[:HALF], h[HALF:]]), (mirror, w0[h[HALF:], h[:HALF]])):
        rows += [x, zero[:HALF]] * 4 + [zero[:HALF], x] * 4

    def pack(x):
        return np.concatenate(x).reshape(FULL + 2, P, CIN).transpose(1, 0, 2)

    def four_times(x):
        padded = np.concatenate([x, np.zeros((P // 4 - x.shape[0], x.shape[1]), x.dtype)])
        return np.tile(padded, (4, 1)).reshape(P, -1, P)

    def by_rows(x):
        return x.reshape(-1, P, x.shape[1] // P, P).transpose(1, 0, 2, 3).reshape(P, -1, P)

    wt1 = np.asarray(inputs["W_top1"])
    return {
        "tables": np.concatenate(tables),
        "ids": ids.reshape(groups, GROUP, n).transpose(1, 2, 0).reshape(P, groups),
        "table_starts": np.repeat(np.tile(starts, GROUP)[:, None], TB, 1),
        "w0_direct": pack(direct),
        "w0_mirror": pack(mirror),
        "w1": np.asarray(inputs["L0_rec_W1"]),
        "dense": four_times(np.asarray(inputs["dense_ctx"]).T),
        "topw": np.concatenate([by_rows(wt1[:2 * P]), by_rows(np.asarray(inputs["W_top2"]))], axis=1),
        "wt1_dense": four_times(wt1[2 * P:]),
        "b1": np.asarray(inputs["b_top1"]).reshape(-1, P).T,
        "b2": np.asarray(inputs["b_top2"]).reshape(-1, P).T,
        "wt3": np.asarray(inputs["W_top3"]).reshape(-1, P).T,
    }


def kernel(**inputs):
    import numpy as np
    import concourse.bacc as bacc
    from concourse.bass_utils import run_bass_kernel_spmd

    nc = bacc.Bacc("TRN2", target_bir_lowering=False, num_devices=1)
    arrays, args = {}, []
    for name, a in laid_out(inputs).items():
        a = np.ascontiguousarray(a)
        arrays[f"in_{name}"] = a
        args.append(nc.dram_tensor(f"in_{name}", a.shape, mybir.dt.from_np(a.dtype), kind="ExternalInput").ap())
    batch = inputs["ids"].shape[0]
    out = nc.dram_tensor("out_y", (P, batch // P), F32, kind="ExternalOutput").ap()
    scratch = nc.dram_tensor("scratch", (RING, 2 * FIELDS, COLS), F32, kind="Internal").ap()
    interaction_tower(nc, *args, scratch, out)
    r = run_bass_kernel_spmd(nc, [arrays], core_ids=[0])
    return r.results[0]["out_y"].T.reshape(batch, 1)
```

```python
from contextlib import ExitStack

import concourse.bass as bass
from concourse import mybir

F32 = mybir.dt.float32
F32R = mybir.dt.float32r
I32 = mybir.dt.int32
U32 = mybir.dt.uint32
ALU = mybir.AluOpType
ACT = mybir.ActivationFunctionType

P = 128
FIELDS = 32
DIM = 32
GROUP = P // FIELDS
HALF = FIELDS // 2
WRAP = FIELDS + HALF // 2
CIN = 128
TB = 4
COLS = TB * P
FULL = 4
UNITS = 3
RING = 4
BDW = FIELDS + 1
NHID1, NHID2 = 512, 256
TOPW = (2 * P * NHID1 + NHID1 * NHID2) // P // P


def interaction_tower(nc, tables, ids, w0_direct, w0_mirror, w1, dense, topw, wt1_dense, last_small, scratch, out):
    nb = ids.shape[1] // TB - 1
    turns = nb // RING
    batch = nb * TB * GROUP
    assert ids.shape[0] == P and nb % RING == 0 and batch == 512

    ctx = ExitStack()
    with ctx:
        def sb(name, shape, dt=F32):
            return ctx.enter_context(nc.sbuf_tensor(name, shape, dt))

        def ps(name, shape):
            return ctx.enter_context(nc.psum_tensor(name, shape, F32))

        def sem(name):
            return ctx.enter_context(nc.semaphore(name))

        ids_raw = sb("ids_raw", [P, (nb + 1) * TB], I32)
        idx = sb("idx", [P, RING, TB], I32)
        emb = sb("emb", [P, RING, TB, DIM])
        embT = sb("embT", [P, RING, TB, WRAP])
        pairs = sb("pairs", [P, 2, 3, COLS])
        zA = sb("zA", [P, 2, TB, 2, P])
        zB = sb("zB", [P, 2, 2, COLS])
        zC = sb("zC", [P, 2, TB, HALF])
        z16 = sb("z16", [P, 2, TB // 2, P])
        zh = sb("zh", [P, 2, FULL, COLS], F32R)
        zl = sb("zl", [P, 2, FULL, COLS], F32R)
        z16s = sb("z16s", [P, 2, TB // 2, P], F32R)
        x1c = sb("x1c", [P, COLS])
        x1 = sb("x1", [P, 2, TB, CIN])
        bd = sb("bd", [P, RING, TB, GROUP, BDW])
        G = sb("G", [P, BDW, batch])
        ident = sb("ident", [P, P])
        w0h = sb("w0h", [P, FULL + 2, CIN], F32R)
        w0l = sb("w0l", [P, FULL, CIN], F32R)
        w1h = sb("w1h", [P, FIELDS, CIN], F32R)
        w1l = sb("w1l", [P, FIELDS, CIN], F32R)
        topw_h = sb("topw_h", [P, TOPW, P], F32R)
        topw_l = sb("topw_l", [P, TOPW, P], F32R)
        wt1d = sb("wt1d", [P, NHID1 // P, P], F32R)
        small = sb("small", [P, (NHID1 + 2 * NHID2) // P])
        b1s, b2s, wt3s = small[:, 0:4], small[:, 4:6], small[:, 6:8]
        dense4 = sb("dense4", [P, NHID1 // P, P], F32R)

        topw_raw = G[:, 0:TOPW, 3 * P:4 * P]
        w0_raw = G[:, 24:30, 2 * P:3 * P]
        w0m_raw = G[:, 24:30, P:2 * P]
        w1_parts = [(0, 8, zA[:, 0, :, :, :].rearrange("p t c n -> p (t c) n")),
                    (8, 20, pairs[:, 0, :, :].rearrange("p a (b n) -> p (a b) n", n=P)),
                    (20, FIELDS, pairs[:, 1, :, :].rearrange("p a (b n) -> p (a b) n", n=P))]
        wt1d_raw = zB[:, 0, 0, :].rearrange("p (c n) -> p c n", n=P)
        dense4_raw = zB[:, 0, 1, :].rearrange("p (c n) -> p c n", n=P)
        hidden1 = zA[:, :, :, :, :].rearrange("p s t c n -> p (s t c n)").rearrange("p (c n) -> p c n", n=batch)
        hidden2 = zB[:, 0, :, :]
        ys = zB[:, 1, 0, 0:batch // P]
        high = zh[:, :, :, :].rearrange("p s c n -> p (s c) n")
        low = zl[:, :, :, :].rearrange("p s c n -> p (s c) n")
        S1, X2 = 4, 5
        Gh = zh[:, 0, :, :].rearrange("p c (g n) -> p (c g) n", g=2)
        Gl = zl[:, 0, :, :].rearrange("p c (g n) -> p (c g) n", g=2)
        G_SLOTS = 8
        G_TERMS = 2 * FIELDS

        def G_term(n):
            return G[:, n % FIELDS, n // FIELDS * batch // 2:(n // FIELDS + 1) * batch // 2]

        zAT = ps("zAT", [P, 2, COLS])
        z16T = ps("z16T", [P, 2, COLS // 2])
        x1T_ps = ps("x1T_ps", [P, 2, COLS])
        x1_ps = ps("x1_ps", [P, TB, CIN])
        G_ps = ps("G_ps", [P, 2, 512])

        hid1_ps = [zAT[:, 0, :], zAT[:, 1, :], z16T[:, :, :].rearrange("p c n -> p (c n)"), x1T_ps[:, 1, :]]

        ids_in = sem("ids_in")
        idx_made = sem("idx_made")
        first_gathered = [sem(f"first_gathered{t}") for t in range(TB)]
        first_turned = sem("first_turned")
        gathered = [sem(f"gathered{n}") for n in range(RING)]
        turned = sem("turned")
        emb_ready = sem("emb_ready")
        written = [sem(f"written{n}") for n in range(2)]
        pairs_ready = [sem(f"pairs_ready{n}") for n in range(2)]
        bd_zero = sem("bd_zero")
        bd_ones = sem("bd_ones")
        bd_ready = [sem(f"bd_ready{n}") for n in range(2)]
        ident_zero = sem("ident_zero")
        ident_ready = sem("ident_ready")
        w0_in = sem("w0_in")
        w0_summed = sem("w0_summed")
        w0_high = sem("w0_high")
        w0_ready = sem("w0_ready")
        w1_in = [sem(f"w1_in{n}") for n in range(3)]
        w1_high = sem("w1_high")
        w1_low = sem("w1_low")
        topw_in = sem("topw_in")
        topw_high = sem("topw_high")
        topw_low = sem("topw_low")
        small_in = sem("small_in")
        small_high = sem("small_high")
        small_low = sem("small_low")
        late_in = sem("late_in")
        zA_made = sem("zA_made")
        zB_made = sem("zB_made")
        zC_made = sem("zC_made")
        z16_made = sem("z16_made")
        zT_made = sem("zT_made")
        zh_made = sem("zh_made")
        zl_made = sem("zl_made")
        x1T_made = sem("x1T_made")
        x1c_made = sem("x1c_made")
        x1_turned = sem("x1_turned")
        x1_made = sem("x1_made")
        G_made = sem("G_made")
        G_kept = sem("G_kept")
        Gh_made = sem("Gh_made")
        Gl_made = sem("Gl_made")
        s1h_made = sem("s1h_made")
        s1l_made = sem("s1l_made")
        x2_terms = sem("x2_terms")
        x2h_made = sem("x2h_made")
        x2l_made = sem("x2l_made")
        hid1_made = sem("hid1_made")
        hid1_kept = sem("hid1_kept")
        hid1h_made = sem("hid1h_made")
        hid1l_made = sem("hid1l_made")
        hid2_made = sem("hid2_made")
        hid2_kept = sem("hid2_kept")
        y_made = sem("y_made")
        y_kept = sem("y_kept")
        y_out = sem("y_out")

        def wait_from_one(eng, semaphore, count):
            if not (isinstance(count, int) and count <= 0):
                eng.wait_ge(semaphore, count)

        def block_before(turn, q, n):
            return turn + (q - n) // RING, (q - n) % RING

        TOPW_PARTS = 4
        assert TOPW_PARTS < turns - 2

        def topw_part(part):
            n = TOPW // TOPW_PARTS
            return bass.ds((part - 1) * n, n)

        block = ctx.enter_context(nc.Block())

        @block.sync
        def _(sp):
            sp.dma_start(ids_raw[:, :], ids).then_inc(ids_in, 16)
            sp.dma_start(w0_raw, w0_direct).then_inc(w0_in, 16)
            sp.dma_start(w0m_raw, w0_mirror).then_inc(w0_in, 16)

            def write(turn, q):
                for copy in range(2):
                    if copy == 0:
                        if isinstance(turn, int) and turn + q == 0:
                            for t in range(TB):
                                sp.wait_ge(first_gathered[t], 16)
                        else:
                            sp.wait_ge(gathered[q], 16 * TB * (turn + (q > 0)))
                    else:
                        wait_from_one(sp, zB_made, turn * RING + q - 1)
                    rows = slice(FIELDS * copy, FIELDS * (copy + 1))
                    sp.dma_start(scratch[q, rows, :].rearrange("h (i n) -> i h n", i=GROUP),
                                 emb[:, q, :, :].rearrange("p t d -> p (t d)")).then_inc(written[q % 2], 16)

            def read(turn, q):
                sp.wait_ge(written[q % 2], 32 * (2 * turn + q // 2 + 1))
                block_ = scratch[q, :, :]
                for at, first, step_, runs in ((0, 0, 0, 1), (1, 8, 2, 2)):
                    src = bass.AP(tensor=block_.tensor, offset=block_.offset + first * COLS,
                                  ap=[[COLS, FIELDS], [step_ * COLS, 4], [1, runs * COLS]])
                    sp.dma_start(pairs[:, q % 2, at:at + runs, :].rearrange("p c n -> p (c n)"), src).then_inc(pairs_ready[q % 2], 16)

            def spread(turn, q):
                if q % 2 == 0:
                    wait_from_one(sp, G_made, turn * RING + q - 4)
                first = (q - q % 2 - 2) % RING
                for i in range(q % 2 * 2, q % 2 * 2 + 2):
                    part = slice(i * DIM, (i + 1) * DIM)
                    sp.dma_start(bd[part, first:first + 2, :, i, 0:FIELDS], embT[part, first:first + 2, :, 0:FIELDS]) \
                        .then_inc(bd_ready[first // 2], 16)

            def step(turn, q, first=False):
                write(turn, q)
                if not (first and q < 2):
                    spread(turn, q)
                read(turn, q)

            for q in range(RING):
                if q == 2:
                    sp.wait_ge(bd_zero, 1)
                step(0, q, first=True)

            def load_topw(part):
                at = topw_part(part)
                sp.dma_start(topw_raw[:, at, :], topw[:, at, :]).then_inc(topw_in, 16)

            with sp.Fori(1, 2) as turn:
                for q in range(RING):
                    step(turn, q)
            load_topw(1)
            with sp.Fori(2, TOPW_PARTS + 1) as turn:
                for q in range(RING):
                    step(turn, q)
                sp.wait_ge(topw_high, turn - 1)
                load_topw(turn)
            with sp.Fori(TOPW_PARTS + 1, turns) as turn:
                for q in range(RING):
                    step(turn, q)

            def load_w1(part):
                first, end, raw = w1_parts[part]
                sp.dma_start(raw, w1.rearrange("(h m) j -> m h j", m=P)[:, first:end, :]).then_inc(w1_in[part], 16)

            sp.wait_ge(zT_made, 2 * (nb - 2) + 1)
            load_w1(0)
            sp.wait_ge(zB_made, nb - 1)
            spread(turns, 0)
            spread(turns, 1)
            load_w1(1)
            sp.wait_ge(zl_made, UNITS * (nb - 1))
            sp.dma_start(wt1d_raw, wt1_dense).then_inc(small_in, 16)
            sp.dma_start(dense4_raw, dense).then_inc(small_in, 16)
            sp.wait_ge(zB_made, nb)
            load_w1(2)
            sp.dma_start(small[:, :], last_small).then_inc(late_in, 16)
            sp.wait_ge(y_kept, 1)
            sp.dma_start(out, ys).then_inc(y_out, 16)
            sp.wait_ge(y_out, 16)

        @block.gpsimd
        def _(pool):
            nc.gpsimd.memset(ident[:, :], 0.0).then_inc(ident_zero, 1)
            pool.wait_ge(ident_zero, 1)
            nc.gpsimd.affine_select(out=ident[:, :], in_=ident[:, :], compare_op=ALU.not_equal, fill=1.0,
                                    base=0, pattern=[[-1, P]], channel_multiplier=1).then_inc(ident_ready, 1)
            pool.wait_ge(ids_in, 16)

            def rows_of(turn, q):
                at = bass.ds((turn * RING + q) * TB, TB)
                nc.gpsimd.tensor_tensor(idx[:, q % RING, :], ids_raw[:, at], ids_raw[:, nb * TB:(nb + 1) * TB], ALU.add).then_inc(idx_made, 1)

            def products_16(turn, q):
                s = turn * RING + q
                pool.wait_ge(emb_ready, s + 1)
                wait_from_one(pool, z16_made, s - 1)
                nc.gpsimd.tensor_tensor(zC[:, q % 2, :, :], embT[:, q, :, 0:HALF], embT[:, q, :, HALF:FIELDS], ALU.mult).then_inc(zC_made, 1)

            def gather(turn, q, last=False):
                wait_from_one(pool, turned, turn * RING + q - 2)
                wait_from_one(pool, written[q % 2], 32 * (2 * turn + q // 2 - 1))
                pool.wait_ge(idx_made, turn * RING + q + 1)
                if not last:
                    rows_of(turn, q + 1)
                for t in range(TB):
                    done = first_gathered[t] if isinstance(turn, int) and turn + q == 0 else gathered[q]
                    nc.gpsimd.indirect_dma_start(
                        emb[:, q, t, :], None, tables,
                        bass.IndirectOffsetOnAxis(ap=idx[:, q, t:t + 1].bitcast(U32), axis=0),
                    ).then_inc(done, 16)

            rows_of(0, 0)
            gather(0, 0)
            gather(0, 1)
            products_16(0, 0)
            gather(0, 2)
            gather(0, 3)

            def gather_turn(turn):
                for q in range(RING):
                    products_16(*block_before(turn, q, 3))
                    gather(turn, q)

            with pool.Fori(1, 2) as turn:
                gather_turn(turn)
            with pool.Fori(2, TOPW_PARTS + 2) as turn:
                gather_turn(turn)
                pool.wait_ge(topw_high, turn - 1)
                at = topw_part(turn - 1)
                nc.gpsimd.tensor_tensor(topw_l[:, at, :], topw_raw[:, at, :], topw_h[:, at, :].bitcast(F32), ALU.subtract).then_inc(topw_low, 1)
            with pool.Fori(TOPW_PARTS + 2, turns - 1) as turn:
                gather_turn(turn)
            for q in range(RING):
                products_16(*block_before(turns - 1, q, 3))
                gather(turns - 1, q, last=(q == RING - 1))
            for q in range(1, RING):
                products_16(turns - 1, q)
            for n, (first, end, raw) in enumerate(w1_parts):
                pool.wait_ge(w1_high, n + 1)
                nc.gpsimd.tensor_tensor(w1l[:, first:end, :], raw, w1h[:, first:end, :].bitcast(F32), ALU.subtract).then_inc(w1_low, 1)
            pool.wait_ge(small_high, 2)
            for n, (p, at, raw) in enumerate(((32, wt1d, wt1d_raw), (96, wt1d, wt1d_raw), (64, dense4, dense4_raw))):
                rows = slice(p, p + 64 if at is dense4 else p + 32)
                pool.wait_ge(*((small_low, n) if n > 0 else (w1_low, 3)))
                nc.gpsimd.tensor_tensor(at[rows, :, :], raw[rows, :, :], at[rows, :, :].bitcast(F32), ALU.subtract).then_inc(small_low, 1)

        @block.vector
        def _(dve):
            def turn_emb(turn, q):
                slot, turn_ = q % RING, turn + q // RING
                dve.wait_ge(gathered[slot], 16 * TB * (turn_ + (slot > 0)))
                wait_from_one(dve, bd_ready[slot // 2], 16 * GROUP * turn_)
                nc.vector.transpose(embT[:, slot, :, 0:FIELDS], emb[:, slot, :, :]).then_inc(turned, 1)

            def products_A(turn, q, gathers=range(TB)):
                slot, first, n = q % RING, gathers[0], len(gathers)
                e = embT[:, slot, first:first + n, :]
                field = bass.AP(tensor=e.tensor, offset=e.offset, ap=[e.ap[0], [WRAP, n], [0, 8], [1, FIELDS]])
                other = bass.AP(tensor=e.tensor, offset=e.offset, ap=[e.ap[0], [WRAP, n], [1, 8], [1, FIELDS]])
                out = zA[:, q % 2, first:first + n, :, :].rearrange("p t c (k h) -> p t (c k) h", h=FIELDS)
                return nc.vector.tensor_tensor(out, field, other, ALU.mult)

            def products_B(turn, q):
                dve.wait_ge(pairs_ready[q % 2], 16 * 2 * (2 * turn + q // 2 + 1))
                for c in range(2):
                    last = nc.vector.tensor_tensor(
                        zB[:, q % 2, c, :].rearrange("p (t i d) -> p t i d", t=TB, i=GROUP),
                        pairs[:, q % 2, 0, :].rearrange("p (i t d) -> p t i d", t=TB, i=GROUP),
                        pairs[:, q % 2, 1 + c, :].rearrange("p (i t d) -> p t i d", t=TB, i=GROUP), ALU.mult)
                last.then_inc(zB_made, 1)

            def first_block():
                for t in range(TB):
                    dve.wait_ge(first_gathered[t], 16)
                    nc.vector.transpose(embT[:, 0, t, 0:FIELDS], emb[:, 0, t, :]).then_inc(turned if t == TB - 1 else first_turned, 1)
                    if t < TB - 1:
                        dve.wait_ge(first_turned, 2 * t + 1)
                    else:
                        dve.wait_ge(turned, 1)
                    nc.vector.tensor_copy(embT[:, 0, t, FIELDS:WRAP], embT[:, 0, t, 0:WRAP - FIELDS]) \
                        .then_inc(emb_ready if t == TB - 1 else first_turned, 1)
                    if t < TB - 1:
                        dve.wait_ge(first_turned, 2 * t + 2)
                    else:
                        dve.wait_ge(emb_ready, 1)
                    last = products_A(0, 0, range(t, t + 1))
                    if t == TB - 1:
                        last.then_inc(zA_made, 1)

            def low_parts(turn, q, unit):
                s = turn * RING + q
                dve.wait_ge(zh_made, UNITS * s + "ACB".index(unit) + 1)
                wait_from_one(dve, x1T_made, s - 1)
                if unit == "C":
                    low, z_, high_ = z16s[64:P, q % 2, :, :], z16T[64:P, 0, :].rearrange("p (u n) -> p u n", n=P), z16s[64:P, q % 2, :, :]
                else:
                    at = slice(0, 2) if unit == "A" else slice(2, 4)
                    low, z_, high_ = zl[:, q % 2, at, :], zAT[:, :, :] if unit == "A" else zB[:, q % 2, :, :], zh[:, q % 2, at, :]
                nc.vector.tensor_tensor(low, z_, high_.bitcast(F32), ALU.subtract).then_inc(zl_made, 1)

            def step(turn, q, first=False, last=False):
                early = first and q == 0
                if early:
                    low_parts(turn, q, "A")
                if not (last and q == RING - 1):
                    dve.wait_ge(emb_ready, turn * RING + q + 2)
                    wait_from_one(dve, zT_made, 2 * (turn * RING + q) - 1)
                    products_A(turn + (q + 1) // RING, (q + 1) % RING).then_inc(zA_made, 1)
                products_B(turn, q)
                if not early:
                    low_parts(turn, q, "A")
                low_parts(turn, q, "C")
                if not (last and q >= RING - 2):
                    turn_emb(turn + (q + 2) // RING, (q + 2) % RING)
                low_parts(turn, q, "B")

            nc.vector.memset(bd[:, :, :, :, :], 0.0).then_inc(bd_zero, 1)
            first_block()
            dve.wait_ge(w0_in, 32)
            nc.vector.tensor_tensor(w0_raw, w0_raw, w0m_raw, ALU.add).then_inc(w0_summed, 1)
            dve.wait_ge(w0_high, 1)
            nc.vector.tensor_tensor(w0l[:, :, :], w0_raw[:, 0:FULL, :], w0h[:, 0:FULL, :].bitcast(F32), ALU.subtract).then_inc(w0_ready, 1)
            for p in (32, 96):
                at = w0h[p:p + 32, FULL:FULL + 2, :]
                nc.vector.tensor_tensor(at, w0_raw[p:p + 32, FULL:FULL + 2, :], at.bitcast(F32), ALU.subtract).then_inc(w0_ready, 1)
            turn_emb(0, 1)
            dve.wait_ge(turned, 2)
            nc.vector.tensor_copy(embT[:, 1, :, FIELDS:WRAP], embT[:, 1, :, 0:WRAP - FIELDS]).then_inc(emb_ready, 1)
            dve.wait_ge(bd_zero, 1)
            for i in range(GROUP):
                nc.vector.memset(bd[i * DIM:(i + 1) * DIM, :, :, i, FIELDS:BDW], 1.0).then_inc(bd_ones, 1)
            for q in range(RING):
                step(0, q, first=True)
            with dve.Fori(1, turns - 1) as turn:
                for q in range(RING):
                    step(turn, q)
            for q in range(RING):
                step(turns - 1, q, last=True)

            def w1_high_part(n):
                first, end, raw = w1_parts[n]
                dve.wait_ge(w1_in[n], 16)
                nc.vector.tensor_copy(w1h[:, first:end, :], raw).then_inc(w1_high, 1)

            def G_low(first, end):
                for n in range(first, end):
                    dve.wait_ge(Gh_made, n + 1)
                    nc.vector.tensor_tensor(Gl[:, n % G_SLOTS, :], G_term(n), Gh[:, n % G_SLOTS, :].bitcast(F32), ALU.subtract).then_inc(Gl_made, 1)

            w1_high_part(0)
            w1_high_part(1)
            G_low(0, 4)
            w1_high_part(2)
            G_low(4, G_TERMS)
            dve.wait_ge(s1h_made, 1)
            nc.vector.tensor_tensor(low[:, S1, :], G[:, FIELDS, :], high[:, S1, :].bitcast(F32), ALU.subtract).then_inc(s1l_made, 1)
            dve.wait_ge(x2h_made, 1)
            nc.vector.tensor_tensor(low[:, X2, :], x1T_ps[:, 0, :], high[:, X2, :].bitcast(F32), ALU.subtract).then_inc(x2l_made, 1)
            for c in range(NHID1 // P):
                dve.wait_ge(hid1_kept, c + 1)
                nc.vector.tensor_copy(high[:, c, :], hidden1[:, c, :]).then_inc(hid1h_made, 1)
                dve.wait_ge(hid1h_made, c + 1)
                nc.vector.tensor_tensor(low[:, c, :], hidden1[:, c, :], high[:, c, :].bitcast(F32), ALU.subtract).then_inc(hid1l_made, 1)
            dve.wait_ge(y_made, 1)
            nc.vector.tensor_copy(ys, x1_ps[:, 0, 0:batch // P]).then_inc(y_kept, 1)

        @block.scalar
        def _(act):
            act.wait_ge(w0_summed, 1)
            nc.scalar.activation(w0h[:, :, :], w0_raw, ACT.Copy).then_inc(w0_high, 1)

            def high_parts(turn, q, unit):
                s = turn * RING + q
                if unit == "B":
                    act.wait_ge(zB_made, s + 1)
                else:
                    act.wait_ge(zT_made, 2 * s + "AC".index(unit) + 1)
                wait_from_one(act, x1T_made, s - 1)
                if unit == "A":
                    out, z_ = zh[:, q % 2, 0:2, :], zAT[:, :, :]
                elif unit == "B":
                    out, z_ = zh[:, q % 2, 2:4, :], zB[:, q % 2, :, :]
                else:
                    out, z_ = z16s[:, q % 2, :, :], z16T[:, 0, :].rearrange("p (u n) -> p u n", n=P)
                nc.scalar.activation(out, z_, ACT.Copy).then_inc(zh_made, 1)

            def keep_x1c(turn, q):
                s = turn * RING + q
                act.wait_ge(x1T_made, s)
                wait_from_one(act, x1_turned, s - 1)
                nc.scalar.activation(x1c[:, :], x1T_ps[:, (q - 1) % 2, :], ACT.Copy).then_inc(x1c_made, 1)

            def keep_x1(turn, q):
                s = turn * RING + q
                act.wait_ge(x1_turned, s - 1)
                wait_from_one(act, G_made, s - 3)
                nc.scalar.activation(x1[:, q % 2, :, :], x1_ps[:, :, :], ACT.Copy).then_inc(x1_made, 1)

            def keep_G(turn, q):
                s = turn * RING + q
                act.wait_ge(G_made, s - 1)
                nc.scalar.activation(
                    G[:, :, bass.ds((s - 2) * TB * GROUP, TB * GROUP)].rearrange("m h (u v) -> m u v h", u=2),
                    G_ps[:, :, 0:2 * GROUP * BDW].rearrange("m u (v h) -> m u v h", h=BDW),
                    ACT.Copy).then_inc(G_kept, 1)

            def wrap(turn, q):
                act.wait_ge(turned, turn * RING + q + 1)
                slot = q % RING
                nc.scalar.activation(embT[:, slot, :, FIELDS:WRAP], embT[:, slot, :, 0:WRAP - FIELDS], ACT.Copy).then_inc(emb_ready, 1)

            def copies_16(turn, q):
                s = turn * RING + q
                act.wait_ge(zC_made, s + 1)
                wait_from_one(act, zT_made, 2 * (s - 1))
                once = zC[:, q % 2, :, :]
                copies = bass.AP(tensor=once.tensor, offset=once.offset, ap=[once.ap[0], [2 * HALF, TB // 2], [0, 4], [1, 2 * HALF]])
                nc.scalar.activation(z16[:, q % 2, :, :].rearrange("p u (c n) -> p u c n", c=4), copies, ACT.Copy).then_inc(z16_made, 1)

            def step(turn, q, first=False, last=False):
                high_parts(turn, q, "A")
                if not (first and q < 2):
                    keep_x1(turn, q)
                high_parts(turn, q, "C")
                high_parts(turn, q, "B")
                if not (first and q < 1):
                    keep_x1c(turn, q)
                if not (first and q < 2):
                    keep_G(turn, q)
                if not (last and q >= RING - 2):
                    wrap(turn, q + 2)
                if not (last and q == RING - 1):
                    copies_16(turn + (q + 1) // RING, (q + 1) % RING)

            copies_16(0, 0)
            for q in range(RING):
                step(0, q, first=True)
            with act.Fori(1, 2) as turn:
                for q in range(RING):
                    step(turn, q)
            with act.Fori(2, TOPW_PARTS + 2) as turn:
                act.wait_ge(topw_in, 16 * (turn - 1))
                at = topw_part(turn - 1)
                nc.scalar.activation(topw_h[:, at, :], topw_raw[:, at, :], ACT.Copy).then_inc(topw_high, 1)
                for q in range(RING):
                    step(turn, q)
            with act.Fori(TOPW_PARTS + 2, turns - 1) as turn:
                for q in range(RING):
                    step(turn, q)
            for q in range(RING):
                step(turns - 1, q, last=True)

            def G_high(first, end):
                for n in range(first, end):
                    if n == 0:
                        act.wait_ge(x1T_made, nb - 1)
                        act.wait_ge(G_kept, nb // 2)
                    if n == FIELDS:
                        act.wait_ge(G_kept, nb)
                    if n >= G_SLOTS:
                        act.wait_ge(x2_terms, n - G_SLOTS + 1)
                    nc.scalar.activation(Gh[:, n % G_SLOTS, :], G_term(n), ACT.Copy).then_inc(Gh_made, 1)

            G_high(0, 2)
            keep_x1(turns, 0)
            G_high(2, 6)
            keep_x1c(turns, 0)
            G_high(6, 7)
            keep_G(turns, 0)
            keep_x1(turns, 1)
            act.wait_ge(small_in, 32)
            nc.scalar.activation(wt1d[:, :, :], wt1d_raw, ACT.Copy).then_inc(small_high, 1)
            nc.scalar.activation(dense4[:, :, :], dense4_raw, ACT.Copy).then_inc(small_high, 1)
            G_high(7, 8)
            keep_G(turns, 1)
            G_high(8, G_TERMS)
            nc.scalar.activation(high[:, S1, :], G[:, FIELDS, :], ACT.Copy).then_inc(s1h_made, 1)
            act.wait_ge(x2_terms, G_TERMS)
            nc.scalar.activation(high[:, X2, :], x1T_ps[:, 0, :], ACT.Copy).then_inc(x2h_made, 1)
            act.wait_ge(late_in, 16)
            for n in range(NHID1 // P):
                act.wait_ge(hid1_made, n + 1)
                nc.scalar.activation(hidden1[:, n, :], hid1_ps[n], ACT.Relu, bias=b1s[:, n:n + 1]).then_inc(hid1_kept, 1)
            for n in range(NHID2 // P):
                act.wait_ge(hid2_made, n + 1)
                nc.scalar.activation(hidden2[:, n, :], G_ps[:, n, :], ACT.Relu, bias=b2s[:, n:n + 1]).then_inc(hid2_kept, 1)

        @block.tensor
        def _(pe):
            def turn_A(turn, q):
                s = turn * RING + q
                pe.wait_ge(zA_made, s + 1)
                wait_from_one(pe, zl_made, UNITS * (s - 1) + 1)
                for c in range(2):
                    for t in range(TB):
                        last = nc.tensor.transpose(zAT[:, c, t * P:(t + 1) * P], zA[:, q % 2, t, c, :], ident[:, :])
                last.then_inc(zT_made, 1)

            def turn_C(turn, q):
                s = turn * RING + q
                pe.wait_ge(z16_made, s + 1)
                wait_from_one(pe, zl_made, UNITS * (s - 1) + 2)
                for t in range(TB // 2):
                    last = nc.tensor.transpose(z16T[:, 0, t * P:(t + 1) * P], z16[:, q % 2, t, :], ident[:, :])
                last.then_inc(zT_made, 1)

            def interact(turn, q, unit):
                s = turn * RING + q
                slot = (q - 1) % 2
                pe.wait_ge(zl_made, UNITS * (s - 1) + "ACB".index(unit) + 1)
                if unit == "A":
                    wait_from_one(pe, x1c_made, s - 2)
                if unit == "C":
                    for t in range(2):
                        nc.tensor.matmul(
                            x1T_ps[:, slot, :].rearrange("j (u t n) -> j u t n", u=2, t=2)[:, :, t, :],
                            w0h[:, FULL + t, :], z16s[:, slot, :, :], start=False, stop=False)
                else:
                    for c in (0, 1) if unit == "A" else (2, 3):
                        for k, (w, half) in enumerate([(w0h, zh), (w0h, zl), (w0l, zh)]):
                            last = nc.tensor.matmul(x1T_ps[:, slot, :], w[:, c, :], half[:, slot, c, :],
                                                    start=(c == 0 and k == 0), stop=(c == 3 and k == 2))
                    if unit == "B":
                        last.then_inc(x1T_made, 1)

            def turn_x1(turn, q):
                s = turn * RING + q
                pe.wait_ge(x1c_made, s - 1)
                wait_from_one(pe, x1_made, s - 2)
                for t in range(TB):
                    last = nc.tensor.transpose(x1_ps[:, t, :], x1c[:, t * P:(t + 1) * P], ident[:, :])
                last.then_inc(x1_turned, 1)

            def dot(turn, q):
                s = turn * RING + q
                slot = (q - 2) % RING
                pe.wait_ge(x1_made, s - 1)
                pe.wait_ge(bd_ready[slot // 2], 16 * GROUP * (turn + q // 2))
                wait_from_one(pe, G_kept, s - 2)
                for t in range(TB):
                    v = t % 2 * GROUP * BDW
                    last = nc.tensor.matmul(G_ps[:, t // 2, v:v + GROUP * BDW], x1[:, q % 2, t, :],
                                            bd[:, slot, t, :, :].rearrange("p i h -> p (i h)"), start=True, stop=True)
                last.then_inc(G_made, 1)

            def step(turn, q, first=False):
                started = not (first and q < 1)
                early = first and q == 1
                if early:
                    interact(turn, q, "A")
                turn_A(turn, q)
                if not (first and q < 2):
                    turn_x1(turn, q)
                if started and not early:
                    interact(turn, q, "A")
                turn_C(turn, q)
                if started:
                    interact(turn, q, "C")
                    interact(turn, q, "B")
                if not (first and q < 2):
                    dot(turn, q)

            pe.wait_ge(ident_ready, 1)
            for q in range(RING):
                if q == 1:
                    pe.wait_ge(w0_ready, 3)
                if q == 2:
                    pe.wait_ge(bd_ones, GROUP)
                step(0, q, first=True)
            with pe.Fori(1, turns) as turn:
                for q in range(RING):
                    step(turn, q)

            def products_of_halves(out, wh, wl, high_, low_, start, stop):
                nc.tensor.matmul(out, wh, high_, start=start, stop=False)
                nc.tensor.matmul(out, wl, high_, start=False, stop=False)
                return nc.tensor.matmul(out, wh, low_, start=False, stop=stop)

            def x2_term(first, end):
                for n in range(first, end):
                    h, g = n % FIELDS, n // FIELDS
                    for part, (field, _, _) in enumerate(w1_parts):
                        if n == field:
                            pe.wait_ge(w1_low, part + 1)
                    pe.wait_ge(Gl_made, n + 1)
                    products_of_halves(x1T_ps[:, 0, g * batch // 2:(g + 1) * batch // 2], w1h[:, h, :], w1l[:, h, :],
                                       Gh[:, n % G_SLOTS, :], Gl[:, n % G_SLOTS, :], h == 0, h == FIELDS - 1).then_inc(x2_terms, 1)

            turn_x1(turns, 0)
            for unit in "ACB":
                interact(turns, 0, unit)
            dot(turns, 0)
            turn_x1(turns, 1)
            x2_term(0, 2)
            dot(turns, 1)
            x2_term(2, G_TERMS)
            pe.wait_ge(s1l_made, 1)
            pe.wait_ge(topw_low, TOPW_PARTS)
            pe.wait_ge(small_low, 3)
            for n, bank in enumerate(hid1_ps):
                products_of_halves(bank, topw_h[:, n, :], topw_l[:, n, :], high[:, S1, :], low[:, S1, :], True, False)
                nc.tensor.matmul(bank, wt1d[:, n, :], dense4[:, :, :].rearrange("p c n -> p (c n)"), start=False, stop=False)
            pe.wait_ge(x2l_made, 1)
            for n, bank in enumerate(hid1_ps):
                products_of_halves(bank, topw_h[:, 4 + n, :], topw_l[:, 4 + n, :], high[:, X2, :], low[:, X2, :], False, True).then_inc(hid1_made, 1)
            for c in range(NHID1 // P):
                pe.wait_ge(hid1l_made, c + 1)
                for n in range(NHID2 // P):
                    last = products_of_halves(G_ps[:, n, :], topw_h[:, 8 + 2 * c + n, :], topw_l[:, 8 + 2 * c + n, :], high[:, c, :], low[:, c, :],
                                              c == 0, c == NHID1 // P - 1)
                    if c == NHID1 // P - 1:
                        last.then_inc(hid2_made, 1)
            pe.wait_ge(late_in, 16)
            pe.wait_ge(hid2_kept, NHID2 // P)
            for k in range(batch // P):
                for c in range(NHID2 // P):
                    last = nc.tensor.matmul(x1_ps[:, 0, k:k + 1], hidden2[:, c, k * P:(k + 1) * P], wt3s[:, c:c + 1],
                                            start=(c == 0), stop=(c == NHID2 // P - 1))
            last.then_inc(y_made, 1)


def laid_out(inputs):
    import numpy as np

    n = FIELDS
    ids = np.asarray(inputs["ids"])
    tables = [np.asarray(inputs[f"tbl_{f}"]) for f in range(n)]
    starts = np.concatenate([[0], np.cumsum([t.shape[0] for t in tables])[:-1]]).astype(np.int32)
    groups = ids.shape[0] // GROUP
    w0 = np.asarray(inputs["L0_rec_W0"]).reshape(n, n, CIN)
    h = np.arange(n)
    zero = np.zeros((n, CIN), np.float32)
    direct = [w0[h, (h + k) % n] for k in range(HALF)]
    mirror = [zero] + [w0[(h + k) % n, h] for k in range(1, HALF)]
    for rows in (direct, mirror):
        rows[8:] = [np.stack(rows[8 + c::2], axis=1).reshape(4 * n, CIN) for c in range(2)]
    for rows, x in ((direct, w0[h[:HALF], h[HALF:]]), (mirror, w0[h[HALF:], h[:HALF]])):
        rows += [x, zero[:HALF]] * 4 + [zero[:HALF], x] * 4

    def pack(x):
        return np.concatenate(x).reshape(FULL + 2, P, CIN).transpose(1, 0, 2)

    def four_times(x):
        padded = np.concatenate([x, np.zeros((P // 4 - x.shape[0], x.shape[1]), x.dtype)])
        return np.tile(padded, (4, 1)).reshape(P, -1, P)

    def by_rows(x):
        return x.reshape(-1, P, x.shape[1] // P, P).transpose(1, 0, 2, 3).reshape(P, -1, P)

    wt1 = np.asarray(inputs["W_top1"])
    return {
        "tables": np.concatenate(tables),
        "ids": np.concatenate([ids.reshape(groups, GROUP, n).transpose(1, 2, 0).reshape(P, groups),
                               np.repeat(np.tile(starts, GROUP)[:, None], TB, 1)], axis=1),
        "w0_direct": pack(direct),
        "w0_mirror": pack(mirror),
        "w1": np.asarray(inputs["L0_rec_W1"]),
        "dense": four_times(np.asarray(inputs["dense_ctx"]).T),
        "topw": np.concatenate([by_rows(wt1[:2 * P]), by_rows(np.asarray(inputs["W_top2"]))], axis=1),
        "wt1_dense": four_times(wt1[2 * P:]),
        "last_small": np.concatenate([np.asarray(inputs[x]).reshape(-1, P).T for x in ("b_top1", "b_top2", "W_top3")], axis=1),
    }


def kernel(**inputs):
    import numpy as np
    import concourse.bacc as bacc
    from concourse.bass_utils import run_bass_kernel_spmd

    nc = bacc.Bacc("TRN2", target_bir_lowering=False, num_devices=1)
    arrays, args = {}, []
    for name, a in laid_out(inputs).items():
        a = np.ascontiguousarray(a)
        arrays[f"in_{name}"] = a
        args.append(nc.dram_tensor(f"in_{name}", a.shape, mybir.dt.from_np(a.dtype), kind="ExternalInput").ap())
    batch = inputs["ids"].shape[0]
    out = nc.dram_tensor("out_y", (P, batch // P), F32, kind="ExternalOutput").ap()
    scratch = nc.dram_tensor("scratch", (RING, 2 * FIELDS, COLS), F32, kind="Internal").ap()
    interaction_tower(nc, *args, scratch, out)
    r = run_bass_kernel_spmd(nc, [arrays], core_ids=[0])
    return r.results[0]["out_y"].T.reshape(batch, 1)
```
